# Optimizing a Trainium2 kernel written in Bass

```python
import numpy as np
import jax
import jax.numpy as jnp

def _softmax(x, axis=-1):
    return jax.nn.softmax(x, axis=axis)

def _gelu(x):
    return jax.nn.gelu(x, approximate=True)

def _silu(x):
    return jax.nn.silu(x)

def _sigmoid(x):
    return jax.nn.sigmoid(x)

def _layernorm(x, axis=-1, eps=1e-05):
    m = jnp.mean(x, axis=axis, keepdims=True)
    v = jnp.var(x, axis=axis, keepdims=True)
    return (x - m) / jnp.sqrt(v + eps)

def _scatter_add(tgt, idx, src, axis=0):
    return tgt.at[idx].add(src)

def _segment_sum(src, seg, n):
    return jax.ops.segment_sum(src, seg, n)
kernel_name = 'mk_gnn_resnorm_d1_gnn_r64_4a1ac7'

def setup_inputs(seed: int=0):
    np.random.seed(seed)
    _w = jnp.asarray

    def _rec_inputs():
        import jax
        import jax.numpy as jnp
        _gk = jax.random.key(seed)
        x = -0.0006008 + 1.001 * jax.random.normal(jax.random.fold_in(_gk, 1), (100000, 256), jnp.float32)
        src = jax.random.randint(jax.random.fold_in(_gk, 2), (25000,), 0, 100000, jnp.int32)
        dst = jnp.minimum((100000 * jax.random.uniform(jax.random.fold_in(_gk, 3), (25000,)) ** 2.0).astype(jnp.int32), 99999)
        _o = jnp.argsort(dst, stable=True)
        src = src[_o]
        dst = dst[_o]
        return (x, src, dst)
    x, src, dst = _rec_inputs()

    def _L0_gnn_setup():
        import jax, jax.numpy as jnp
        import numpy as np
        N, E, D = (10000, 5000, 256)
        key = jax.random.key(seed)
        k1, k2, k3, k4 = jax.random.split(key, 4)
        x = jax.random.normal(k1, (N, D), dtype=jnp.float32)
        edge_index = jax.random.randint(k2, (2, E), 0, N, dtype=jnp.int64)
        s = 1.0 / np.sqrt(D)
        w1 = jax.random.uniform(k3, (D, D), dtype=jnp.float32, minval=-s, maxval=s)
        b1 = jnp.zeros((D,), dtype=jnp.float32)
        w2 = jax.random.uniform(k4, (D, D), dtype=jnp.float32, minval=-s, maxval=s)
        b2 = jnp.zeros((D,), dtype=jnp.float32)
        return {'x': x, 'edge_index': edge_index, 'w1': w1, 'b1': b1, 'w2': w2, 'b2': b2}
    _L0_gnn_all = _L0_gnn_setup()
    _L0_gnn_in = {k: v for k, v in _L0_gnn_all.items() if k in ('w1', 'b1', 'w2', 'b2')}
    del _L0_gnn_all
    return {'x': x, 'src': src, 'dst': dst, 'L0_gnn_w1': _L0_gnn_in['w1'], 'L0_gnn_b1': _L0_gnn_in['b1'], 'L0_gnn_w2': _L0_gnn_in['w2'], 'L0_gnn_b2': _L0_gnn_in['b2']}

def reference(x, src, dst, L0_gnn_w1, L0_gnn_b1, L0_gnn_w2, L0_gnn_b2):
    import jax
    import jax.numpy as jnp

    def _L0_gnn_ref(x, edge_index, w1, b1, w2, b2):
        import jax, jax.numpy as jnp
        import numpy as np
        N, E, D = (10000, 5000, 256)

        def mlp(h):
            return jax.nn.relu(h @ w1 + b1) @ w2 + b2
        row, col = (edge_index[0], edge_index[1])
        msgs = mlp(x[col])
        agg = jax.ops.segment_sum(msgs, row, num_segments=x.shape[0])
        return mlp(x + agg)
    edge_index = jnp.stack([src, dst])
    x = _layernorm(x + _L0_gnn_ref(x, edge_index, L0_gnn_w1, L0_gnn_b1, L0_gnn_w2, L0_gnn_b2), axis=-1)
    return x

_drawn_inputs = setup_inputs


def setup_inputs(seed=0):
    import zlib

    import numpy as np

    out = dict(_drawn_inputs(seed))
    spreads = {'L0_gnn_b1': (0.0, 0.1), 'L0_gnn_b2': (0.0, 0.1)}
    factors = {}
    for name, (base, spread) in spreads.items():
        noise = np.random.default_rng([zlib.crc32(name.encode()), seed]).standard_normal(out[name].shape)
        drawn = base * np.exp(spread * noise) if base else spread * noise
        out[name] = jnp.asarray(drawn.astype(out[name].dtype))
    for name, factor in factors.items():
        out[name] = (out[name] * factor).astype(out[name].dtype)
    return out
```

```python
from contextlib import ExitStack

import concourse.bass as bass
from concourse import mybir

P = 128
ALU = mybir.AluOpType
ACT = mybir.ActivationFunctionType
F32 = mybir.dt.float32
F32R = mybir.dt.float32r
BF16 = mybir.dt.bfloat16
F16 = mybir.dt.float16
I32 = mybir.dt.int32

U = 6


class Step:

    def __init__(self, turn, k):
        self.turn, self.k = turn, k

    def plus(self, n):
        return Step(self.turn, self.k + n)

    def slot(self, slots):
        return self.k % slots

    def within(self, groups):
        return not isinstance(self.turn, int) or 0 <= self.k < groups

    def has(self, n):
        if isinstance(self.turn, int):
            return self.k >= n
        assert U + self.k >= n, "not so in the loop's first turn"
        return True

    def loops(self):
        return not isinstance(self.turn, int)

    def last(self, groups):
        return isinstance(self.turn, int) and self.k == groups - 1

    def times(self, per, more=0):
        return self.turn * (U * per) + (self.k * per + more)

    def visits(self, slots, per):
        return self.turn * (U // slots * per) + (self.k // slots + 1) * per


def steps(engine, body, groups, ahead, behind):
    turns = (groups - ahead) // U
    for n in range(-ahead, U):
        body(Step(0, n))
    with engine.Fori(1, turns) as turn:
        for k in range(U):
            body(Step(turn, k))
    for n in range(turns * U, groups + behind):
        body(Step(0, n))


def gnn_kernel(nc, x, src, dst, w1, b1, w2, b2, out):
    N, D = x.shape
    E, = src.shape
    KD = D // P
    J = 4
    ROWS = J * P
    EG = -(-E // ROWS)
    EP = EG * ROWS
    ET = EG * J
    NG = -(-N // ROWS)
    TAIL = (N - (NG - 1) * ROWS) // J
    NC = NG * J
    QE = 2 * P
    Q = EP // QE
    CH = EP // 32
    SHIFT_P, SHIFT_G = 2, 9
    EPS = 1e-5
    assert D == KD * P and J == 1 << SHIFT_P and ROWS == 1 << SHIFT_G and TAIL * J == N - (NG - 1) * ROWS
    assert Q <= P and EP % 32 == 0 and NG * ROWS > N

    with ExitStack() as ctx:
        def sb(name, shape, dt=F32):
            return ctx.enter_context(nc.sbuf_tensor(name, shape, dt))

        def sem(name):
            return ctx.enter_context(nc.semaphore(name))

        def ps(name, shape, dt=F32):
            return ctx.enter_context(nc.psum_tensor(name, shape, dt))

        src_sorted = nc.dram_tensor("src_sorted", (EP,), I32, kind="Internal").ap()
        dst_sorted = nc.dram_tensor("dst_sorted", (EP,), I32, kind="Internal").ap()
        same_row = nc.dram_tensor("same_row", (EP,), F32, kind="Internal").ap()
        agg_rows = nc.dram_tensor("agg_rows", (EP, D), F32, kind="Internal").ap()

        NX, NA, NY, NM, NO = U, 3, 3, 3, 2

        w1f, w2f = sb("w1f", [P, KD, D]), sb("w2f", [P, KD, D])
        w1h, w1l = sb("w1h", [P, KD, D], F32R), sb("w1l", [P, KD, D], F32R)
        w2h, w2l = sb("w2h", [P, KD, D], F32R), sb("w2l", [P, KD, D], F32R)
        b1c = sb("b1c", [P, KD])
        b2row = sb("b2row", [P, D])
        b2parts = sb("b2parts", [P, D], F32R)
        ones = sb("ones", [P, P], F32R)
        onesf = sb("onesf", [P, P])
        below = sb("below", [P, P])
        ident = sb("ident", [P, P])
        b2zero = sb("b2zero", [P, D])
        b2high = sb("b2high", [P, D], F32R)
        onesc = onesf[:, 0:1]
        eps = sb("eps", [P, 1])
        iota_p = sb("iota_p", [P, P], F16)
        iota_c = sb("iota_c", [P, NC], F16)
        iota_i = sb("iota_i", [P, max(NC, P)], I32)

        src_pm, dst_pm, prev_pm = (sb(n, [P, ET], I32) for n in ("src_pm", "dst_pm", "prev_pm"))
        drop_pm = sb("drop_pm", [P, ET])
        drops = sb("drops", [P, 1])
        drops_int = sb("drops_int", [P, 1], I32)
        src_q, dst_q, prev_q = (sb(n, [P, QE], I32) for n in ("src_q", "dst_q", "prev_q"))
        src_qf, dst_qf, same_q = (sb(n, [P, QE]) for n in ("src_qf", "dst_qf", "same_q"))
        run_q = sb("run_q", [P, QE])
        edge_q, edge_qi = sb("edge_q", [P, QE]), sb("edge_qi", [P, QE], I32)
        start_q = sb("start_q", [P, QE])
        carry_col, carry_row, carry_scan = sb("carry_col", [P, P]), sb("carry_row", [P, P]), sb("carry_scan", [P, P])
        src_t = sb("src_t", [P, ET], I32)
        dst_t = sb("dst_t", [P, ET], I32)
        cnt_t = sb("cnt_t", [P, ET])
        part_i, col_i, col_lo = (sb(n, [P, ET], I32) for n in ("part_i", "col_i", "col_lo"))
        part_t, col_t = sb("part_t", [P, ET]), sb("col_t", [P, ET])

        count = sb("count", [P, NG, J])
        upto = sb("upto", [P, NG, J])
        group_sum = sb("group_sum", [P, NG])
        src_now = sb("src_now", [P, NX, J], I32)
        row_now = sb("row_now", [P, 3, J], I32)
        onesg = sb("onesg", [P, NG])
        group_scan = sb("group_scan", [P, NG])
        base = sb("base", [P, NG])
        rowf = sb("rowf", [P, NG, J])
        row_idx = sb("row_idx", [P, NC], I32)

        chunk_i, chunk_f, chunk_eq = sb("chunk_i", [P, CH], I32), sb("chunk_f", [P, CH]), sb("chunk_eq", [P, CH])
        chunk_iota = sb("chunk_iota", [P, CH])
        edge_no = sb("edge_no", [P, ET])
        edge_no_i = sb("edge_no_i", [P, ET], I32)
        dst_pmf = sb("dst_pmf", [P, ET])
        rank = sb("rank", [P, ET])
        rank_i = sb("rank_i", [P, ET], I32)
        one_dst, one_no = sb("one_dst", [P, 1]), sb("one_no", [P, 1])
        rank_one, src_one, dst_one = (sb(n, [P, 1], I32) for n in ("rank_one", "src_one", "dst_one"))
        less, ties = sb("less", [P, 1]), sb("ties", [P, 1])

        xs = sb("xs", [P, NX, J, D])
        aggs = sb("aggs", [P, NA, J, D])
        xa = sb("xa", [P, 2, J, D])
        xth, xtl = sb("xth", [P, 2, KD, ROWS], F32R), sb("xtl", [P, 2, KD, ROWS], F32R)
        hid = sb("hid", [P, 2, KD, ROWS])
        hsum = sb("hsum", [P, 2, KD, ROWS])
        hh, hl = sb("hh", [P, 2, KD, ROWS], F32R), sb("hl", [P, 2, KD, ROWS], F32R)
        same = sb("same", [P, NM, ROWS])
        onep, onec = sb("onep", [P, NO, J, P], BF16), sb("onec", [P, NO, J, NC], BF16)
        ys = sb("ys", [P, NY, J, D])
        sq = sb("sq", [P, J, D])
        ysum, nmean, ysq = sb("ysum", [P, NY, J]), sb("nmean", [P, NY, J]), sb("ysq", [P, NY, J])
        std, rstd = sb("std", [P, NY, J]), sb("rstd", [P, NY, J])

        xt_ps = ps("xt_ps", [P, KD, ROWS])
        hid_ps = ps("hid_ps", [P, KD, ROWS])
        out_ps = ps("out_ps", [P, J, D])
        cnt_ps = ps("cnt_ps", [P, 2, ROWS])
        HC = NC // 2

        s_pads = sem("s_pads")
        s_weights, s_lists = sem("s_weights"), sem("s_lists")
        s_const, s_iota, s_split = sem("s_const"), sem("s_iota"), sem("s_split")
        s_drop, s_drop_sum, s_drop_int = sem("s_drop"), sem("s_drop_sum"), sem("s_drop_int")
        s_padded = sem("s_padded")
        r_iota, r_chunk, r_chunk_used, r_step, r_ranks, r_one, r_scatter = (
            sem("r_iota"), sem("r_chunk"), sem("r_chunk_used"), sem("r_step"), sem("r_ranks"), sem("r_one"),
            sem("r_scatter"))
        s_ordered = sem("s_ordered")
        s_rows, s_row_ops, s_row_turned, s_row_copied, s_cols = (
            sem("s_rows"), sem("s_row_ops"), sem("s_row_turned"), sem("s_row_copied"), sem("s_cols"))
        s_same_out = sem("s_same_out")
        e_idx = sem("e_idx")
        r_issue, e_issue, n_issue = sem("r_issue"), sem("e_issue"), sem("n_issue")
        e_x = [sem(f"e_x{n}") for n in range(NX)]
        e_same = [sem(f"e_same{n}") for n in range(NM)]
        e_turned, e_high, e_xt = sem("e_turned"), sem("e_high"), sem("e_xt")
        e_layer1, e_relu, e_scan, e_hh, e_hl = sem("e_layer1"), sem("e_relu"), sem("e_scan"), sem("e_hh"), sem("e_hl")
        e_layer2, e_agg = sem("e_layer2"), sem("e_agg")
        e_stored = [sem(f"e_stored{n}") for n in range(NY)]
        e_onehot, e_counted = sem("e_onehot"), sem("e_counted")
        t_ops, t_sums, t_rows = sem("t_ops"), sem("t_sums"), sem("t_rows")
        n_x = [sem(f"n_x{n}") for n in range(NX)]
        n_zero = sem("n_zero")
        n_agg = [sem(f"n_agg{n}") for n in range(NA)]
        n_xa, n_turned, n_high, n_xt = sem("n_xa"), sem("n_turned"), sem("n_high"), sem("n_xt")
        n_layer1, n_relu, n_hh, n_hl, n_layer2 = (
            sem("n_layer1"), sem("n_relu"), sem("n_hh"), sem("n_hl"), sem("n_layer2"))
        n_y, n_nmean, n_sq, n_std, n_rstd, n_out = (
            sem("n_y"), sem("n_nmean"), sem("n_sq"), sem("n_std"), sem("n_rstd"), sem("n_out"))
        n_stored = [sem(f"n_stored{n}") for n in range(NY)]

        block = ctx.enter_context(nc.Block())

        full = N - (NG - 1) * ROWS
        x_groups = x[0:(NG - 1) * ROWS, :].rearrange("(g p j) d -> g p j d", p=P, j=J)
        out_groups = out[0:(NG - 1) * ROWS, :].rearrange("(g p j) d -> g p j d", p=P, j=J)
        x_tail = x[N - full:N, :].rearrange("(p j) d -> p j d", j=J)
        out_tail = out[N - full:N, :].rearrange("(p j) d -> p j d", j=J)
        agg_groups = agg_rows.rearrange("(g j p) d -> g p j d", p=P, j=J)
        same_groups = same_row.rearrange("(g r) -> g r", r=ROWS)

        dst_chunks = dst_sorted.rearrange("(c r) -> c r", r=CH)

        def columns(table, step):
            i = step.times(J)
            return table[:, i:i + J] if isinstance(i, int) else table[:, bass.ds(i, J)]

        def group(view, step):
            i = step.times(1)
            return view[i] if isinstance(i, int) else view[bass.ds(i, 1)].rearrange("a p j d -> p (a j) d")

        @block.sync
        def _(sp):
            sp.wait_ge(s_pads, 1)
            whole = E // ET
            rest = E - whole * ET
            for tile, lst in ((src_pm, src), (dst_pm, dst)):
                sp.dma_start(tile[0:whole, :], lst[0:whole * ET].rearrange("(p t) -> p t", t=ET)).then_inc(s_lists, 16)
                sp.dma_start(tile[whole:whole + 1, 0:rest], lst[whole * ET:E].rearrange("(p t) -> p t", p=1)).then_inc(s_lists, 16)
            one = dst.rearrange("(a e) -> a e", a=1)
            sp.dma_start(prev_pm[0:1, 1:ET], one[:, 0:ET - 1]).then_inc(s_lists, 16)
            sp.dma_start(prev_pm[1:whole, :], dst[ET - 1:whole * ET - 1].rearrange("(p t) -> p t", t=ET)).then_inc(s_lists, 16)
            sp.dma_start(prev_pm[whole:whole + 1, 0:rest + 1], one[:, whole * ET - 1:E]).then_inc(s_lists, 16)
            for tile, w in ((w1f, w1), (w2f, w2)):
                sp.dma_start(tile[:], w.rearrange("(k p) n -> p k n", p=P)).then_inc(s_weights, 16)
            for k in range(KD):
                sp.dma_start(b1c[:, k:k + 1], b1[k * P:(k + 1) * P].rearrange("(p a) -> p a", a=1)).then_inc(s_weights, 16)
            sp.dma_start(b2row[:], b2.rearrange("(a n) -> a n", a=1).broadcast_to([P, D])).then_inc(s_weights, 16)
            sp.wait_ge(s_lists, 16 * 7)
            sp.dma_start(src_sorted.rearrange("(p t) -> p t", t=ET), src_pm[:]).then_inc(s_padded, 16)
            sp.dma_start(dst_sorted.rearrange("(p t) -> p t", t=ET), dst_pm[:]).then_inc(s_padded, 16)
            sp.wait_ge(s_ordered, 1)
            sp.dma_start(src_q[0:Q, :], src_sorted.rearrange("(q r) -> q r", r=QE)).then_inc(s_rows, 16)
            sp.dma_start(dst_q[0:Q, :], dst_sorted.rearrange("(q r) -> q r", r=QE)).then_inc(s_rows, 16)
            line = dst_sorted.rearrange("(a e) -> a e", a=1)
            sp.dma_start(prev_q[0:1, 1:QE], line[:, 0:QE - 1]).then_inc(s_rows, 16)
            sp.dma_start(prev_q[1:Q, :], dst_sorted[QE - 1:EP - 1].rearrange("(q r) -> q r", r=QE)).then_inc(s_rows, 16)
            sp.wait_ge(s_row_ops, 2)
            sp.dma_start(same_row.rearrange("(q r) -> q r", r=QE), same_q[0:Q, :]).then_inc(s_same_out, 16)
            sp.wait_ge(s_same_out, 16)

            def edges(i):
                if i.has(0) and i.within(EG):
                    if i.has(NM):
                        sp.wait_ge(e_scan, i.times(KD, KD * (1 - NM)))
                    n = i.slot(NM)
                    g = i.times(1)
                    row = same_groups[g:g + 1, :] if isinstance(g, int) else same_groups[bass.ds(g, 1), :]
                    sp.dma_start(same[:, n, :], row.broadcast_to([P, ROWS])).then_inc(e_same[n], 16)
                m = i.plus(-NM)
                if m.has(0) and m.within(EG):
                    sp.wait_ge(e_agg, m.times(1, 1))
                    sp.dma_start(group(agg_groups, m), ys[:, m.slot(NY), :, :]).then_inc(e_stored[m.slot(NY)], 16)

            steps(sp, edges, EG, 1, NM)

            def nodes(i):
                if i.has(0) and i.within(NG):
                    n = i.slot(NX)
                    if i.has(NX):
                        sp.wait_ge(n_y, i.times(1, 1 - NX))
                    elif i.k == 0:
                        sp.wait_ge(e_turned, EG)
                    if i.last(NG):
                        sp.dma_start(xs[0:TAIL, n, :, :], x_tail).then_inc(n_x[n], 16)
                    else:
                        sp.dma_start(xs[:, n, :, :], group(x_groups, i)).then_inc(n_x[n], 16)
                m = i.plus(-NX)
                if m.has(0) and m.within(NG):
                    sp.wait_ge(n_out, m.times(1, 1))
                    if m.last(NG):
                        sp.dma_start(out_tail, ys[0:TAIL, m.slot(NY), :, :]).then_inc(n_stored[m.slot(NY)], 16)
                    else:
                        sp.dma_start(group(out_groups, m), ys[:, m.slot(NY), :, :]).then_inc(n_stored[m.slot(NY)], 16)

            steps(sp, nodes, NG, 1, NX)
            for n in range(NY):
                sp.wait_ge(n_stored[n], 16 * len(range(n, NG, NY)))

        @block.gpsimd
        def _(pool):
            pool.memset(src_pm[:], 0)
            pool.memset(dst_pm[:], N)
            pool.memset(prev_pm[:], N).then_inc(s_iota, 1)
            pool.wait_ge(s_iota, 1)
            pool.memset(prev_pm[0:1, 0:1], -1)
            pool.memset(prev_q[0:1, 0:1], -1).then_inc(s_pads, 1)
            pool.memset(onesf[:], 1.0)
            pool.memset(eps[:], EPS)
            pool.memset(onesg[:], 1.0)
            pool.memset(ident[:], 0.0)
            pool.memset(carry_col[:], 0.0)
            pool.memset(carry_scan[:], 0.0)
            pool.memset(b2zero[:], 0.0)
            pool.iota(iota_i[:], pattern=[[1, max(NC, P)]], base=0, channel_multiplier=0)
            pool.iota(edge_qi[:], pattern=[[1, QE]], base=0, channel_multiplier=QE)
            pool.iota(edge_no_i[:], pattern=[[1, ET]], base=0, channel_multiplier=ET).then_inc(s_iota, 1)
            pool.wait_ge(s_iota, 2)
            pool.affine_select(out=ident[:], in_=ident[:], compare_op=ALU.not_equal, fill=1.0, base=0,
                               pattern=[[-1, P]], channel_multiplier=1)
            pool.affine_select(out=below[:], in_=onesf[:], compare_op=ALU.is_gt, fill=0.0, base=0,
                               pattern=[[1, P]], channel_multiplier=-1)
            pool.tensor_copy(iota_c[:], iota_i[:, 0:NC])
            pool.tensor_copy(iota_p[:], iota_i[:, 0:P])
            pool.tensor_copy(edge_q[:], edge_qi[:]).then_inc(s_const, 1)

            pool.wait_ge(s_padded, 32)
            pool.wait_ge(s_drop_int, 1)
            dropped = pool.value_load(drops_int[0:1, 0:1], min_val=0, max_val=EP)
            with pool.If(dropped > 0):
                pool.iota(chunk_i[:], pattern=[[1, CH]], base=0, channel_multiplier=0).then_inc(r_iota, 1)
                with pool.Fori(0, EP // CH) as c:
                    pool.wait_ge(r_chunk_used, c + 1)
                    at = dst_chunks[bass.ds(c, 1), :]
                    pool.dma_start(chunk_i[:], at.broadcast_to([P, CH])).then_inc(r_chunk, 16)
                with pool.Fori(0, ET) as t:
                    pool.wait_ge(r_one, t + 1)
                    pool.sem_inc(r_issue, 1)
                    for lst, to in ((src_one, src_sorted), (dst_one, dst_sorted)):
                        pool.indirect_dma_start(
                            to.rearrange("(e a) -> e a", a=1),
                            bass.IndirectOffsetOnAxis(ap=rank_one[:, 0:1], axis=0),
                            lst[:], None).then_inc(r_scatter, 16)
                pool.wait_ge(r_scatter, 32 * ET)
            pool.sem_inc(s_ordered, 1)

            pool.wait_ge(s_cols, 1)

            def edges(i):
                if i.has(0) and i.within(EG):
                    n = i.slot(NX)
                    if i.has(NX):
                        pool.wait_ge(e_turned, i.times(1, 1 - NX))
                        pool.wait_ge(e_x[n], i.plus(-NX).visits(NX, 16 * J))
                    pool.tensor_copy(src_now[:, n, :], columns(src_t, i)).then_inc(e_idx, 1)
                    pool.wait_ge(e_idx, i.times(1, 1))
                    pool.sem_inc(e_issue, 1)
                    for j in range(J):
                        pool.indirect_dma_start(
                            xs[:, n, j, :], None, x,
                            bass.IndirectOffsetOnAxis(ap=src_now[:, n, j:j + 1], axis=0)).then_inc(e_x[n], 16)

            steps(pool, edges, EG, 1, 0)
            pool.wait_ge(t_rows, 1)
            for n in range(NY):
                pool.wait_ge(e_stored[n], 16 * len(range(n, EG, NY)))

            def nodes(i):
                if i.has(0) and i.within(NG):
                    n = i.slot(NA)
                    if i.has(NA):
                        pool.wait_ge(n_xa, i.times(1, 1 - NA))
                    pool.tensor_copy(row_now[:, n, :], columns(row_idx, i))
                    pool.memset(aggs[:, n, :, :], 0.0).then_inc(n_zero, 1)
                    pool.wait_ge(n_zero, i.times(1, 1))
                    pool.sem_inc(n_issue, 1)
                    for j in range(J):
                        pool.indirect_dma_start(
                            aggs[:, n, j, :], None, agg_rows,
                            bass.IndirectOffsetOnAxis(ap=row_now[:, n, j:j + 1], axis=0),
                            bounds_check=EP - 1, oob_is_err=False).then_inc(n_agg[n], 16)

            steps(pool, nodes, NG, 1, 0)

        def transposes(source, n):
            for k in range(KD):
                for j in range(J):
                    last = nc.tensor.transpose(xt_ps[:, k, j * P:(j + 1) * P], source[:, n, j, k * P:(k + 1) * P], ident[:])
            return last

        def layer1(m, n):
            parts = [(w, v, k) for k in range(KD) for w, v in ((w1h, xth), (w1l, xth), (w1h, xtl))]
            for at, (w, v, k) in enumerate(parts):
                last = nc.tensor.matmul(hid_ps[:, m, :], w[:, k, m * P:(m + 1) * P], v[:, n, k, :],
                                        start=(at == 0), stop=(at == len(parts) - 1))
            return last

        def layer2(n, with_b2):
            parts = [(v, w, k) for k in range(KD) for v, w in ((hh, w2h), (hh, w2l), (hl, w2h))]
            for j in range(J):
                if with_b2:
                    nc.tensor.matmul(out_ps[:, j, :], ones[:], b2parts[:], start=True, stop=False)
                for at, (v, w, k) in enumerate(parts):
                    last = nc.tensor.matmul(out_ps[:, j, :], v[:, n, k, j * P:(j + 1) * P], w[:, k, :],
                                            start=(at == 0 and not with_b2), stop=(at == len(parts) - 1))
            return last

        @block.tensor
        def _(pe):
            pe.wait_ge(s_const, 1)
            pe.wait_ge(s_drop, 1)
            pe.matmul(out_ps[:, 0, 0:1], onesf[:], drops[:], start=True, stop=True).then_inc(s_drop_sum, 1)

            pe.wait_ge(s_row_copied, 1)
            pe.transpose(out_ps[:, 0, 0:P], carry_col[:], ident[:]).then_inc(s_row_turned, 1)
            pe.wait_ge(s_row_copied, 2)
            pe.transpose(out_ps[:, 2, 0:P], carry_scan[:], ident[:]).then_inc(s_row_turned, 1)
            pe.wait_ge(s_row_copied, 3)
            for n, rows in enumerate((src_qf, dst_qf, run_q)):
                for h in range(QE // P):
                    last = pe.transpose(xt_ps[:, h, n * Q:(n + 1) * Q], rows[0:Q, h * P:(h + 1) * P], ident[0:Q, 0:Q])
            last.then_inc(s_row_turned, 1)
            pe.wait_ge(s_split, 1)
            pe.wait_ge(s_cols, 1)

            def edges(i):
                j = i.plus(1)
                if j.within(EG):
                    pe.wait_ge(e_x[j.slot(NX)], j.visits(NX, 16 * J))
                    if j.has(1):
                        pe.wait_ge(e_xt, j.times(1))
                    transposes(xs, j.slot(NX)).then_inc(e_turned, 1)
                if i.has(0) and i.within(EG):
                    pe.wait_ge(e_xt, i.times(1, 1))
                    for m in range(KD):
                        if i.has(1):
                            pe.wait_ge(e_relu, i.times(KD, m + 1 - KD))
                        layer1(m, i.slot(2)).then_inc(e_layer1, 1)
                    pe.wait_ge(e_onehot, i.times(1, 1))
                    for j in range(J):
                        for h in range(2):
                            last = pe.matmul(cnt_ps[:, h, 0:HC], onep[:, i.slot(NO), j, :],
                                             onec[:, i.slot(NO), j, h * HC:(h + 1) * HC],
                                             start=(not i.loops() and i.k == 0 and j == 0),
                                             stop=(i.last(EG) and j == J - 1), skip_group_check=True)
                    last.then_inc(e_counted, 1)
                m = i.plus(-2)
                if m.has(0) and m.within(EG):
                    pe.wait_ge(e_hl, m.times(1, 1))
                    if m.has(1):
                        pe.wait_ge(e_agg, m.times(1))
                    layer2(m.slot(2), False).then_inc(e_layer2, 1)

            steps(pe, edges, EG, 1, 2)

            pe.wait_ge(t_sums, 1)
            pe.matmul(xt_ps[:, 0, 0:NG], below[:], group_sum[:], start=True, stop=True)
            pe.matmul(xt_ps[:, 1, 0:NG], onesf[:], group_sum[:], start=True, stop=True).then_inc(t_sums, 1)

            def nodes(i):
                j = i.plus(1)
                if j.within(NG):
                    pe.wait_ge(n_xa, j.times(1, 1))
                    if j.has(1):
                        pe.wait_ge(n_xt, j.times(1))
                    transposes(xa, j.slot(2)).then_inc(n_turned, 1)
                if i.has(0) and i.within(NG):
                    pe.wait_ge(n_xt, i.times(1, 1))
                    for m in range(KD):
                        if i.has(1):
                            pe.wait_ge(n_relu, i.times(KD, m + 1 - KD))
                        layer1(m, i.slot(2)).then_inc(n_layer1, 1)
                m = i.plus(-1)
                if m.has(0) and m.within(NG):
                    pe.wait_ge(n_hl, m.times(1, 1))
                    if m.has(1):
                        pe.wait_ge(n_y, m.times(1))
                    layer2(m.slot(2), True).then_inc(n_layer2, 1)

            steps(pe, nodes, NG, 1, 1)

        @block.scalar
        def _(act):
            act.wait_ge(s_weights, 16 * (3 + KD))

            def edges(i):
                j = i.plus(1)
                if j.within(EG):
                    act.wait_ge(e_turned, j.times(1, 1))
                    if j.has(2):
                        act.wait_ge(e_layer1, j.times(KD, -KD))
                    nc.scalar.copy(xth[:, j.slot(2), :, :], xt_ps[:]).then_inc(e_high, 1)
                m = i.plus(-1)
                if m.has(0) and m.within(EG):
                    act.wait_ge(e_scan, m.times(KD, KD))
                    if m.has(2):
                        act.wait_ge(e_layer2, m.times(1, -1))
                    nc.scalar.copy(hh[:, m.slot(2), :, :], hsum[:, m.slot(2), :, :]).then_inc(e_hh, 1)
                if i.has(0) and i.within(EG):
                    for m in range(KD):
                        act.wait_ge(e_layer1, i.times(KD, m + 1))
                        if i.has(2):
                            act.wait_ge(e_scan, i.times(KD, m + 1 - 2 * KD))
                        nc.scalar.activation(hid[:, i.slot(2), m, :], hid_ps[:, m, :], ACT.Relu,
                                             bias=b1c[:, m:m + 1]).then_inc(e_relu, 1)

            steps(act, edges, EG, 1, 2)

            def nodes(i):
                j = i.plus(1)
                if j.within(NG):
                    act.wait_ge(n_turned, j.times(1, 1))
                    if j.has(2):
                        act.wait_ge(n_layer1, j.times(KD, -KD))
                    nc.scalar.copy(xth[:, j.slot(2), :, :], xt_ps[:]).then_inc(n_high, 1)
                m = i.plus(-2)
                if m.has(0) and m.within(NG):
                    n = m.slot(NY)
                    act.wait_ge(n_nmean, m.times(1, 1))
                    if m.has(1):
                        act.wait_ge(n_sq, m.times(J))
                    for j in range(J):
                        nc.scalar.activation(sq[:, j, :], ys[:, n, j, :], ACT.Square, bias=nmean[:, n, j:j + 1],
                                             accum_out=ysq[:, n, j:j + 1]).then_inc(n_sq, 1)
                    act.wait_ge(n_sq, m.times(J, J))
                    nc.scalar.activation(std[:, n, :], ysq[:, n, :], ACT.Sqrt, bias=eps[:, 0:1],
                                         scale=1.0 / D).then_inc(n_std, 1)
                if i.has(0) and i.within(NG):
                    s = i.slot(2)
                    for m in range(KD):
                        act.wait_ge(n_layer1, i.times(KD, m + 1))
                        if i.has(2):
                            act.wait_ge(n_hl, i.times(1, -1))
                        nc.scalar.activation(hid[:, s, m, :], hid_ps[:, m, :], ACT.Relu,
                                             bias=b1c[:, m:m + 1]).then_inc(n_relu, 1)
                    act.wait_ge(n_relu, i.times(KD, KD))
                    if i.has(2):
                        act.wait_ge(n_layer2, i.times(1, -1))
                    nc.scalar.copy(hh[:, s, :, :], hid[:, s, :, :]).then_inc(n_hh, 1)

            steps(act, nodes, NG, 1, 2)

        @block.vector
        def _(dve):
            chain = [0]

            def then(ins):
                chain[0] += 1
                ins.then_inc(s_row_ops, 1)
                dve.wait_ge(s_row_ops, chain[0])

            dve.wait_ge(s_lists, 16 * 7)
            then(dve.tensor_tensor(drop_pm[:], prev_pm[:], dst_pm[:], ALU.is_gt))
            dve.reduce_sum(drops[:], drop_pm[:], axis=mybir.AxisListType.X).then_inc(s_drop, 1)
            dve.wait_ge(s_drop_sum, 1)
            dve.tensor_copy(drops_int[:], out_ps[:, 0, 0:1]).then_inc(s_drop_int, 1)
            dve.wait_ge(s_drop_int, 1)
            dropped = dve.value_load(drops_int[0:1, 0:1], min_val=0, max_val=EP)
            with dve.If(dropped > 0):
                dve.wait_ge(r_iota, 1)
                dve.tensor_copy(chunk_iota[:], chunk_i[:]).then_inc(r_chunk_used, 1)
                dve.wait_ge(s_const, 1)
                dve.tensor_copy(edge_no[:], edge_no_i[:])
                dve.tensor_copy(dst_pmf[:], dst_pm[:])
                dve.memset(rank[:], 0.0).then_inc(r_ranks, 1)
                dve.wait_ge(r_ranks, 1)
                OPS = 5
                with dve.Fori(0, EP // CH) as c:
                    dve.wait_ge(r_chunk, c * 16 + 16)
                    dve.tensor_copy(chunk_f[:], chunk_i[:]).then_inc(r_chunk_used, 1)
                    with dve.Fori(0, ET) as t:
                        done = c * (ET * OPS) + t * OPS
                        dve.tensor_copy(one_dst[:], dst_pmf[:, bass.ds(t, 1)]).then_inc(r_step, 1)
                        dve.tensor_copy(one_no[:], edge_no[:, bass.ds(t, 1)]).then_inc(r_step, 1)
                        dve.wait_ge(r_step, done + 2)
                        dve.tensor_scalar(chunk_eq[:], chunk_iota[:], one_no[:, 0:1], None, ALU.is_lt).then_inc(r_step, 1)
                        dve.wait_ge(r_chunk_used, c + 2)
                        dve.wait_ge(r_step, done + 3)
                        dve.scalar_tensor_tensor(chunk_eq[:], chunk_f[:], one_dst[:, 0:1], chunk_eq[:], ALU.is_equal,
                                                 ALU.mult, accum_out=ties[:]).then_inc(r_step, 1)
                        dve.wait_ge(r_step, done + 4)
                        dve.scalar_tensor_tensor(chunk_eq[:], chunk_f[:], one_dst[:, 0:1], onesc.broadcast_to([P, CH]),
                                                 ALU.is_lt, ALU.mult, accum_out=less[:]).then_inc(r_step, 1)
                        dve.wait_ge(r_step, done + 5)
                        dve.scalar_tensor_tensor(rank[:, bass.ds(t, 1)], less[:], ties[:, 0:1], rank[:, bass.ds(t, 1)],
                                                 ALU.add, ALU.add).then_inc(r_ranks, 1)
                        dve.wait_ge(r_ranks, c * (ET + 1) + t + 2)
                    dve.tensor_scalar(edge_no[:], edge_no[:], -float(CH), None, ALU.add).then_inc(r_ranks, 1)
                    dve.wait_ge(r_ranks, c * (ET + 1) + (ET + 2))
                dve.tensor_copy(rank_i[:], rank[:]).then_inc(r_ranks, 1)
                dve.wait_ge(r_ranks, EP // CH * (ET + 1) + 2)

                def tile(t):
                    dve.tensor_copy(rank_one[:], rank_i[:, bass.ds(t, 1)])
                    dve.tensor_copy(src_one[:], src_pm[:, bass.ds(t, 1)])
                    dve.tensor_copy(dst_one[:], dst_pm[:, bass.ds(t, 1)]).then_inc(r_one, 1)

                tile(0)
                with dve.Fori(1, ET) as t:
                    dve.wait_ge(r_scatter, t * 32)
                    tile(t)

            dve.wait_ge(s_rows, 64)
            dve.wait_ge(s_const, 1)
            then(dve.tensor_tensor(same_q[0:Q, :], prev_q[0:Q, :], dst_q[0:Q, :], ALU.is_equal))
            then(dve.scalar_tensor_tensor(start_q[0:Q, :], same_q[0:Q, :], 0.0, edge_q[0:Q, :], ALU.is_equal, ALU.mult))
            then(dve.tensor_tensor_scan(run_q[0:Q, :], start_q[0:Q, :], start_q[0:Q, :], 0.0, ALU.max, ALU.max))
            dve.tensor_copy(carry_col[0:Q, 0:1], run_q[0:Q, QE - 1:QE]).then_inc(s_row_copied, 1)
            dve.wait_ge(s_row_turned, 1)
            then(dve.tensor_copy(carry_row[0:1, :], out_ps[0:1, 0, 0:P]))
            dve.tensor_tensor_scan(carry_scan[0:1, 1:P], carry_row[0:1, 0:P - 1], carry_row[0:1, 0:P - 1], 0.0,
                                   ALU.max, ALU.max).then_inc(s_row_copied, 1)
            dve.wait_ge(s_row_turned, 2)
            then(dve.tensor_copy(carry_col[0:Q, 1:2], out_ps[0:Q, 2, 0:1]))
            then(dve.tensor_scalar(run_q[0:Q, :], run_q[0:Q, :], carry_col[0:Q, 1:2], -1.0, ALU.max, ALU.mult))
            then(dve.scalar_tensor_tensor(run_q[0:Q, :], run_q[0:Q, :], 1.0, edge_q[0:Q, :], ALU.add, ALU.add))
            dve.tensor_copy(src_qf[0:Q, :], src_q[0:Q, :])
            dve.tensor_copy(dst_qf[0:Q, :], dst_q[0:Q, :]).then_inc(s_row_copied, 1)
            dve.wait_ge(s_row_turned, 3)
            for n, tiles in enumerate((src_t, dst_t, cnt_t)):
                for h in range(QE // P):
                    last = dve.tensor_copy(tiles[:].rearrange("p (q h) -> p q h", h=QE // P)[:, :, h],
                                           xt_ps[:, h, n * Q:(n + 1) * Q])
            last.then_inc(s_cols, 1)
            dve.wait_ge(s_cols, 1)
            dve.tensor_scalar(part_i[:], dst_t[:], SHIFT_P, P - 1, ALU.logical_shift_right, ALU.bitwise_and)
            dve.tensor_scalar(col_i[:], dst_t[:], SHIFT_G, SHIFT_P, ALU.logical_shift_right, ALU.logical_shift_left)
            then(dve.tensor_scalar(col_lo[:], dst_t[:], J - 1, None, ALU.bitwise_and))
            dve.tensor_copy(part_t[:], part_i[:])
            then(dve.tensor_tensor(col_t[:], col_i[:], col_lo[:], ALU.add))
            dve.wait_ge(s_weights, 16 * (3 + KD))
            dve.tensor_copy(ones[:], onesf[:])
            dve.tensor_copy(w1h[:], w1f[:])
            dve.tensor_copy(w2h[:], w2f[:])
            dve.tensor_copy(b2parts[:], b2zero[:])
            then(dve.tensor_copy(b2high[:], b2row[:]))
            dve.tensor_copy(b2parts[0:1, :], b2row[0:1, :])
            dve.tensor_tensor(b2parts[32:33, :], b2row[32:33, :], b2high[32:33, :].bitcast(F32), ALU.subtract)
            dve.tensor_tensor(w1l[:], w1f[:], w1h[:].bitcast(F32), ALU.subtract)
            dve.tensor_tensor(w2l[:], w2f[:], w2h[:].bitcast(F32), ALU.subtract).then_inc(s_split, 1)

            def edges(i):
                m = i.plus(-3)
                if m.has(0) and m.within(EG):
                    dve.wait_ge(e_layer2, m.times(1, 1))
                    if m.has(NY):
                        dve.wait_ge(e_stored[m.slot(NY)], m.plus(-NY).visits(NY, 16))
                    cnts = columns(cnt_t, m)
                    for j in range(J):
                        last = dve.scalar_tensor_tensor(ys[:, m.slot(NY), j, :], b2row[:], cnts[:, j:j + 1],
                                                        out_ps[:, j, :], ALU.mult, ALU.add)
                    last.then_inc(e_agg, 1)
                m = i.plus(-1)
                if m.has(0) and m.within(EG):
                    s = m.slot(2)
                    dve.wait_ge(e_same[m.slot(NM)], m.visits(NM, 16))
                    if m.has(2):
                        dve.wait_ge(e_hh, m.times(1, -1))
                    for h in range(KD):
                        dve.wait_ge(e_relu, m.times(KD, h + 1))
                        before = 0.0
                        if m.has(1):
                            dve.wait_ge(e_scan, m.times(KD, h + 1 - KD))
                            before = hsum[:, 1 - s, h, ROWS - 1:ROWS]
                        dve.tensor_tensor_scan(hsum[:, s, h, :], same[:, m.slot(NM), :], hid[:, s, h, :], before,
                                               ALU.mult, ALU.add).then_inc(e_scan, 1)
                j = i.plus(1)
                if j.within(EG):
                    if j.has(NO):
                        dve.wait_ge(e_counted, j.times(1, 1 - NO))
                    parts, cols = columns(part_t, j), columns(col_t, j)
                    for t in range(J):
                        dve.tensor_scalar(onep[:, j.slot(NO), t, :], iota_p[:], parts[:, t:t + 1], None, ALU.is_equal)
                        last = dve.tensor_scalar(onec[:, j.slot(NO), t, :], iota_c[:], cols[:, t:t + 1], None, ALU.is_equal)
                    last.then_inc(e_onehot, 1)
                    dve.wait_ge(e_high, j.times(1, 1))
                    dve.tensor_tensor(xtl[:, j.slot(2), :, :], xt_ps[:], xth[:, j.slot(2), :, :].bitcast(F32),
                                      ALU.subtract).then_inc(e_xt, 1)
                if m.has(0) and m.within(EG):
                    dve.wait_ge(e_hh, m.times(1, 1))
                    dve.tensor_tensor(hl[:, s, :, :], hsum[:, s, :, :], hh[:, s, :, :].bitcast(F32),
                                      ALU.subtract).then_inc(e_hl, 1)

            steps(dve, edges, EG, 1, 3)

            chain[0] = 0

            def then(ins):
                chain[0] += 1
                ins.then_inc(t_ops, 1)
                dve.wait_ge(t_ops, chain[0])

            dve.wait_ge(e_counted, EG)
            flat = count[:].rearrange("p g j -> p (g j)")
            dve.tensor_copy(flat[:, 0:HC], cnt_ps[:, 0, 0:HC])
            then(dve.tensor_copy(flat[:, HC:NC], cnt_ps[:, 1, 0:HC]))
            then(dve.tensor_copy(upto[:, :, 0], count[:, :, 0]))
            for j in range(1, J):
                then(dve.tensor_tensor(upto[:, :, j], upto[:, :, j - 1], count[:, :, j], ALU.add))
            dve.tensor_copy(group_sum[:], upto[:, :, J - 1]).then_inc(t_sums, 1)
            then(dve.tensor_scalar(count[:], count[:], 0.0, float(1 << 20), ALU.is_equal, ALU.mult))
            then(dve.scalar_tensor_tensor(rowf[:], upto[:], -1.0, count[:], ALU.add, ALU.add))
            dve.wait_ge(t_sums, 2)
            then(dve.tensor_tensor_scan(group_scan[:], onesg[:], xt_ps[:, 1, 0:NG], 0.0, ALU.mult, ALU.add))
            then(dve.tensor_tensor(base[:], group_scan[:], xt_ps[:, 1, 0:NG], ALU.subtract))
            then(dve.tensor_tensor(base[:], base[:], xt_ps[:, 0, 0:NG], ALU.add))
            for j in range(J):
                last = dve.tensor_tensor(rowf[:, :, j], rowf[:, :, j], base[:], ALU.add)
            then(last)
            dve.tensor_copy(row_idx[:].rearrange("p (g j) -> p g j", j=J), rowf[:]).then_inc(t_rows, 1)

            def nodes(i):
                m = i.plus(-2)
                if m.has(0) and m.within(NG):
                    n = m.slot(NY)
                    dve.wait_ge(n_layer2, m.times(1, 1))
                    if m.has(NY):
                        dve.wait_ge(n_stored[n], m.plus(-NY).visits(NY, 16))
                    for j in range(J):
                        last = dve.scalar_tensor_tensor(ys[:, n, j, :], out_ps[:, j, :], 1.0, xs[:, m.slot(NX), j, :], ALU.mult,
                                                        ALU.add, accum_out=ysum[:, n, j:j + 1])
                    last.then_inc(n_y, 1)
                    dve.wait_ge(n_y, m.times(1, 1))
                    dve.tensor_scalar(nmean[:, n, :], ysum[:, n, :], -1.0 / D, None, ALU.mult).then_inc(n_nmean, 1)
                m = i.plus(-1)
                if m.has(0) and m.within(NG):
                    s = m.slot(2)
                    dve.wait_ge(n_hh, m.times(1, 1))
                    dve.tensor_tensor(hl[:, s, :, :], hid[:, s, :, :], hh[:, s, :, :].bitcast(F32),
                                      ALU.subtract).then_inc(n_hl, 1)
                j = i.plus(1)
                if j.has(0) and j.within(NG):
                    dve.wait_ge(n_high, j.times(1, 1))
                    dve.tensor_tensor(xtl[:, j.slot(2), :, :], xt_ps[:], xth[:, j.slot(2), :, :].bitcast(F32),
                                      ALU.subtract).then_inc(n_xt, 1)
                m = i.plus(-2)
                if m.has(0) and m.within(NG):
                    n = m.slot(NY)
                    dve.wait_ge(n_std, m.times(1, 1))
                    dve.reciprocal(rstd[:, n, :], std[:, n, :]).then_inc(n_rstd, 1)
                    dve.wait_ge(n_rstd, m.times(1, 1))
                    for j in range(J):
                        last = dve.tensor_scalar(ys[:, n, j, :], ys[:, n, j, :], nmean[:, n, j:j + 1], rstd[:, n, j:j + 1],
                                                 ALU.add, ALU.mult)
                    last.then_inc(n_out, 1)
                j = i.plus(2)
                if j.within(NG):
                    dve.wait_ge(n_x[j.slot(NX)], j.visits(NX, 16))
                    dve.wait_ge(n_agg[j.slot(NA)], j.visits(NA, 16 * J))
                    if j.has(2):
                        dve.wait_ge(n_turned, j.times(1, -1))
                    dve.tensor_tensor(xa[:, j.slot(2), :, :], xs[:, j.slot(NX), :, :], aggs[:, j.slot(NA), :, :],
                                      ALU.add).then_inc(n_xa, 1)

            steps(dve, nodes, NG, 2, 2)


_INS = ["x", "src", "dst", "L0_gnn_w1", "L0_gnn_b1", "L0_gnn_w2", "L0_gnn_b2"]


def kernel(**inputs):
    import numpy as _np
    import concourse.bacc as _bacc
    from concourse import mybir as _mybir
    from concourse.bass_utils import run_bass_kernel_spmd as _run

    nc = _bacc.Bacc("TRN2", target_bir_lowering=False, num_devices=1)
    arrays, args = {}, []
    for name in _INS:
        a = _np.ascontiguousarray(inputs[name])
        arrays[f"in_{name}_dram"] = a
        args.append(nc.dram_tensor(f"in_{name}_dram", a.shape, _mybir.dt.from_np(a.dtype), kind="ExternalInput").ap())
    shape = inputs["x"].shape
    args.append(nc.dram_tensor("out_0_dram", shape, F32, kind="ExternalOutput").ap())
    x, src, dst, *rest = args
    gnn_kernel(nc, x, dst, src, *rest)
    r = _run(nc, [arrays], core_ids=[0])
    return r.results[0]["out_0_dram"]
```

```python
from contextlib import ExitStack

import concourse.bass as bass
from concourse import mybir

P = 128
ALU = mybir.AluOpType
ACT = mybir.ActivationFunctionType
F32 = mybir.dt.float32
F32R = mybir.dt.float32r
BF16 = mybir.dt.bfloat16
F16 = mybir.dt.float16
I32 = mybir.dt.int32

U = 6


class Step:

    def __init__(self, turn, k):
        self.turn, self.k = turn, k

    def plus(self, n):
        return Step(self.turn, self.k + n)

    def slot(self, slots):
        return self.k % slots

    def within(self, groups):
        return not isinstance(self.turn, int) or 0 <= self.k < groups

    def has(self, n):
        if isinstance(self.turn, int):
            return self.k >= n
        assert U + self.k >= n, "not so in the loop's first turn"
        return True

    def loops(self):
        return not isinstance(self.turn, int)

    def last(self, groups):
        return isinstance(self.turn, int) and self.k == groups - 1

    def times(self, per, more=0):
        return self.turn * (U * per) + (self.k * per + more)

    def visits(self, slots, per):
        return self.turn * (U // slots * per) + (self.k // slots + 1) * per


def steps(engine, body, groups, ahead, behind):
    turns = (groups - ahead) // U
    for n in range(-ahead, U):
        body(Step(0, n))
    with engine.Fori(1, turns) as turn:
        for k in range(U):
            body(Step(turn, k))
    for n in range(turns * U, groups + behind):
        body(Step(0, n))


def gnn_kernel(nc, x, src, dst, w1, b1, w2, b2, out):
    N, D = x.shape
    E, = src.shape
    KD = D // P
    J = 4
    ROWS = J * P
    EG = -(-E // ROWS)
    EP = EG * ROWS
    ET = EG * J
    NG = -(-N // ROWS)
    TAIL = (N - (NG - 1) * ROWS) // J
    NC = NG * J
    QE = 2 * P
    Q = EP // QE
    SHIFT_P, SHIFT_G = 2, 9
    DIGIT = 8
    LOW = 1 << DIGIT
    CHUNKS = (LOW // P, -(-(N // LOW + 1) // P))
    HOT = max(CHUNKS) * P
    DLOW = 9
    VALS = 4
    EPS = 1e-5
    assert D == KD * P and J == 1 << SHIFT_P and ROWS == 1 << SHIFT_G and TAIL * J == N - (NG - 1) * ROWS
    assert Q <= P and HOT <= 512 and ET * 2 <= 512 and N < 1 << (DLOW + 11) and NG * ROWS > N

    with ExitStack() as ctx:
        def sb(name, shape, dt=F32):
            return ctx.enter_context(nc.sbuf_tensor(name, shape, dt))

        def sem(name):
            return ctx.enter_context(nc.semaphore(name))

        def ps(name, shape, dt=F32):
            return ctx.enter_context(nc.psum_tensor(name, shape, dt))

        src_line = nc.dram_tensor("src_line", (EP,), F32, kind="Internal").ap()
        same_row = nc.dram_tensor("same_row", (EP,), F32, kind="Internal").ap()
        agg_rows = nc.dram_tensor("agg_rows", (EP, D), F32, kind="Internal").ap()

        NX, NA, NY, NM, NO = U, 3, 3, 3, 2

        w1f, w2f = sb("w1f", [P, KD, D]), sb("w2f", [P, KD, D])
        w1h, w1l = sb("w1h", [P, KD, D], F32R), sb("w1l", [P, KD, D], F32R)
        w2h, w2l = sb("w2h", [P, KD, D], F32R), sb("w2l", [P, KD, D], F32R)
        b1c = sb("b1c", [P, KD])
        b2row = sb("b2row", [P, D])
        b2parts = sb("b2parts", [P, D], F32R)
        ones = sb("ones", [P, P], F32R)
        onesf = sb("onesf", [P, P])
        below = sb("below", [P, P])
        ident = sb("ident", [P, P])
        b2zero = sb("b2zero", [P, D])
        b2high = sb("b2high", [P, D], F32R)
        onesc = onesf[:, 0:1]
        eps = sb("eps", [P, 1])
        iota_p = sb("iota_p", [P, P], F16)
        iota_c = sb("iota_c", [P, NC], F16)
        iota_i = sb("iota_i", [P, max(NC, HOT)], I32)

        src_q, dst_q = sb("src_q", [P, QE], I32), sb("dst_q", [P, QE], I32)
        src_qf, dst_qf, same_q, prev_q = (sb(n, [P, QE]) for n in ("src_qf", "dst_qf", "same_q", "prev_q"))
        run_q = sb("run_q", [P, QE])
        edge_q, edge_qi = sb("edge_q", [P, QE]), sb("edge_qi", [P, QE], I32)
        start_q = sb("start_q", [P, QE])
        carry_col, carry_row, carry_scan = sb("carry_col", [P, P]), sb("carry_row", [P, P]), sb("carry_scan", [P, P])
        src_t = sb("src_t", [P, ET], I32)
        dst_t = sb("dst_t", [P, ET], I32)
        srcf_t = sb("srcf_t", [P, ET])
        cnt_t = sb("cnt_t", [P, ET])
        part_i, col_i, col_lo = (sb(n, [P, ET], I32) for n in ("part_i", "col_i", "col_lo"))
        part_t, col_t = sb("part_t", [P, ET]), sb("col_t", [P, ET])

        vals = [sb(f"vals{n}", [P, VALS, ET]) for n in range(3)]
        equal = sb("equal", [P, 2, J, P], BF16)
        place_low, place = sb("place_low", [P, 2, J]), sb("place", [P, 2, J], I32)
        place_i, place_f = sb("place_i", [P, 2, 2, J], I32), sb("place_f", [P, 2, 2, J])
        hot_p = sb("hot_p", [P, 2, J, P], F16)
        digit_total = sb("digit_total", [P, HOT // P])
        digit_base = sb("digit_base", [P, HOT // P])
        starts = sb("starts", [P, HOT // P, ET, 2], BF16)
        belowb, identb = sb("belowb", [P, P], BF16), sb("identb", [P, P], BF16)
        ones_col, low_one = sb("ones_col", [P, 1], BF16), sb("low_one", [P, 2], BF16)
        iota_h = sb("iota_h", [P, HOT], F16)

        count = sb("count", [P, NG, J])
        upto = sb("upto", [P, NG, J])
        group_sum = sb("group_sum", [P, NG])
        dst_now = sb("dst_now", [P, NX, J], I32)
        row_now = sb("row_now", [P, 3, J], I32)
        onesg = sb("onesg", [P, NG])
        onese = sb("onese", [P, ET])
        group_scan = sb("group_scan", [P, NG])
        base = sb("base", [P, NG])
        rowf = sb("rowf", [P, NG, J])
        row_idx = sb("row_idx", [P, NC], I32)

        xs = sb("xs", [P, NX, J, D])
        aggs = sb("aggs", [P, NA, J, D])
        xa = sb("xa", [P, 2, J, D])
        xth, xtl = sb("xth", [P, 2, KD, ROWS], F32R), sb("xtl", [P, 2, KD, ROWS], F32R)
        hid = sb("hid", [P, 2, KD, ROWS])
        hsum = sb("hsum", [P, 2, KD, ROWS])
        hh, hl = sb("hh", [P, 2, KD, ROWS], F32R), sb("hl", [P, 2, KD, ROWS], F32R)
        same = sb("same", [P, NM, ROWS])
        onep, onec = sb("onep", [P, NO, J, P], BF16), sb("onec", [P, NO, J, NC], BF16)
        ys = sb("ys", [P, NY, J, D])
        sq = sb("sq", [P, J, D])
        ysum, nmean, ysq = sb("ysum", [P, NY, J]), sb("nmean", [P, NY, J]), sb("ysq", [P, NY, J])
        std, rstd = sb("std", [P, NY, J]), sb("rstd", [P, NY, J])

        def over(ring, shape, dt, at=0):
            size = 1
            for n in shape:
                size *= n
            flat = ring[:].rearrange("p " + "abc"[:len(ring.shape) - 1].replace("", " ").strip() + " -> p ("
                                     + "abc"[:len(ring.shape) - 1].replace("", " ").strip() + ")").bitcast(dt)
            names = "abcd"[:len(shape)].replace("", " ").strip()
            return flat[:, at:at + size].rearrange(f"p ({names}) -> p {names}", **dict(zip("abcd", shape)))

        hot = over(hsum, [2, J, HOT], BF16)
        hot_turned = over(hid, [2, HOT // P, J * P], BF16)
        hot_t = over(xs, [2, J, VALS, ET], F16)
        vals_i = over(ys, [VALS, ET], I32)
        digit_scan, digit_before = (over(xa, [HOT // P, ET], F32, n * HOT // P * ET) for n in range(2))
        start_i, start_part = (over(aggs, [HOT // P, ET], I32, n * HOT // P * ET) for n in range(2))

        xt_ps = ps("xt_ps", [P, KD, ROWS])
        hid_ps = ps("hid_ps", [P, KD, ROWS])
        out_ps = ps("out_ps", [P, J, D])
        cnt_ps = ps("cnt_ps", [P, 2, ROWS])
        turned_ps = xt_ps[:].rearrange("p k r -> p (k r)").bitcast(BF16).rearrange("p (c r) -> p c r", r=J * P)
        equal_ps = hid_ps[:, 0, :].rearrange("p (j e) -> p j e", j=J)
        place_ps = hid_ps[:, 1, 0:2 * J * 2].rearrange("p (n j v) -> p n j v", n=2, j=J)
        below4 = belowb[:, None, :].broadcast_to([P, J, P])
        moved_ps = out_ps[:].rearrange("p (a b) d -> p a (b d)", a=2)[:, :, 0:2 * ET]

        def digit_count(c, t):
            at = c % 2 * ET + t
            return cnt_ps[:, c // 2, at:at + 1] if isinstance(t, int) else cnt_ps[:, c // 2, bass.ds(at, 1)]

        def start_of(c, t):
            return starts[:, c, t, :] if isinstance(t, int) else starts[:, c, bass.ds(t, 1), :].rearrange("p a v -> p (a v)")
        HC = NC // 2

        s_pads = sem("s_pads")
        s_weights, s_lists = sem("s_weights"), sem("s_lists")
        s_const, s_iota, s_split = sem("s_const"), sem("s_iota"), sem("s_split")
        s_read, s_turned, s_vals = sem("s_read"), sem("s_turned"), sem("s_vals")
        a_hot, a_counted, a_total, a_prefix, a_starts = (
            [sem(f"{n}{d}") for d in range(2)] for n in ("a_hot", "a_counted", "a_total", "a_prefix", "a_starts"))
        b_hot, b_turned, b_copied, b_equal, b_masked, b_place, b_moved, b_moves = (
            [sem(f"{n}{d}") for d in range(2)]
            for n in ("b_hot", "b_turned", "b_copied", "b_equal", "b_masked", "b_place", "b_moved", "b_moves"))
        s_sorted, s_key_rows, s_key_copied, s_line, s_prev = (
            sem("s_sorted"), sem("s_key_rows"), sem("s_key_copied"), sem("s_line"), sem("s_prev"))
        s_sort_ops, b_ops = sem("s_sort_ops"), [sem(f"b_ops{d}") for d in range(2)]
        s_row_ops, s_row_turned, s_row_copied, s_cols = (
            sem("s_row_ops"), sem("s_row_turned"), sem("s_row_copied"), sem("s_cols"))
        s_same_out = sem("s_same_out")
        e_idx = sem("e_idx")
        e_issue, n_issue = sem("e_issue"), sem("n_issue")
        e_x = [sem(f"e_x{n}") for n in range(NX)]
        e_same = [sem(f"e_same{n}") for n in range(NM)]
        e_turned, e_high, e_xt = sem("e_turned"), sem("e_high"), sem("e_xt")
        e_layer1, e_relu, e_scan, e_hh, e_hl = sem("e_layer1"), sem("e_relu"), sem("e_scan"), sem("e_hh"), sem("e_hl")
        e_layer2, e_agg = sem("e_layer2"), sem("e_agg")
        e_stored = [sem(f"e_stored{n}") for n in range(NY)]
        e_onehot, e_counted = sem("e_onehot"), sem("e_counted")
        t_ops, t_sums, t_rows = sem("t_ops"), sem("t_sums"), sem("t_rows")
        n_x = [sem(f"n_x{n}") for n in range(NX)]
        n_zero = sem("n_zero")
        n_agg = [sem(f"n_agg{n}") for n in range(NA)]
        n_xa, n_turned, n_high, n_xt = sem("n_xa"), sem("n_turned"), sem("n_high"), sem("n_xt")
        n_layer1, n_relu, n_hh, n_hl, n_layer2 = (
            sem("n_layer1"), sem("n_relu"), sem("n_hh"), sem("n_hl"), sem("n_layer2"))
        n_y, n_nmean, n_sq, n_std, n_rstd, n_out = (
            sem("n_y"), sem("n_nmean"), sem("n_sq"), sem("n_std"), sem("n_rstd"), sem("n_out"))
        n_stored = [sem(f"n_stored{n}") for n in range(NY)]

        block = ctx.enter_context(nc.Block())

        full = N - (NG - 1) * ROWS
        x_groups = x[0:(NG - 1) * ROWS, :].rearrange("(g p j) d -> g p j d", p=P, j=J)
        out_groups = out[0:(NG - 1) * ROWS, :].rearrange("(g p j) d -> g p j d", p=P, j=J)
        x_tail = x[N - full:N, :].rearrange("(p j) d -> p j d", j=J)
        out_tail = out[N - full:N, :].rearrange("(p j) d -> p j d", j=J)
        agg_groups = agg_rows.rearrange("(g j p) d -> g p j d", p=P, j=J)
        same_groups = same_row.rearrange("(g r) -> g r", r=ROWS)

        def columns(table, step):
            i = step.times(J)
            return table[:, i:i + J] if isinstance(i, int) else table[:, bass.ds(i, J)]

        def group(view, step):
            i = step.times(1)
            return view[i] if isinstance(i, int) else view[bass.ds(i, 1)].rearrange("a p j d -> p (a j) d")

        @block.sync
        def _(sp):
            sp.wait_ge(s_pads, 1)
            whole = E // QE
            rest = E - whole * QE
            for tile, lst in ((src_q, src), (dst_q, dst)):
                sp.dma_start(tile[0:whole, :], lst[0:whole * QE].rearrange("(q r) -> q r", r=QE)).then_inc(s_lists, 16)
                sp.dma_start(tile[whole:whole + 1, 0:rest], lst[whole * QE:E].rearrange("(q r) -> q r", q=1)).then_inc(s_lists, 16)
            for tile, w in ((w1f, w1), (w2f, w2)):
                sp.dma_start(tile[:], w.rearrange("(k p) n -> p k n", p=P)).then_inc(s_weights, 16)
            for k in range(KD):
                sp.dma_start(b1c[:, k:k + 1], b1[k * P:(k + 1) * P].rearrange("(p a) -> p a", a=1)).then_inc(s_weights, 16)
            sp.dma_start(b2row[:], b2.rearrange("(a n) -> a n", a=1).broadcast_to([P, D])).then_inc(s_weights, 16)
            sp.wait_ge(s_key_copied, 1)
            sp.dma_start(src_line.rearrange("(q r) -> q r", r=QE), src_qf[0:Q, :]).then_inc(s_line, 16)
            sp.wait_ge(s_line, 16)
            sp.dma_start(prev_q[0:1, 1:QE], src_line[0:QE - 1].rearrange("(q r) -> q r", q=1)).then_inc(s_prev, 16)
            sp.dma_start(prev_q[1:Q, :], src_line[QE - 1:EP - 1].rearrange("(q r) -> q r", r=QE)).then_inc(s_prev, 16)
            sp.wait_ge(s_row_ops, 1)
            sp.dma_start(same_row.rearrange("(q r) -> q r", r=QE), same_q[0:Q, :]).then_inc(s_same_out, 16)
            sp.wait_ge(s_same_out, 16)

            def edges(i):
                if i.has(0) and i.within(EG):
                    if i.has(NM):
                        sp.wait_ge(e_scan, i.times(KD, KD * (1 - NM)))
                    n = i.slot(NM)
                    g = i.times(1)
                    row = same_groups[g:g + 1, :] if isinstance(g, int) else same_groups[bass.ds(g, 1), :]
                    sp.dma_start(same[:, n, :], row.broadcast_to([P, ROWS])).then_inc(e_same[n], 16)
                m = i.plus(-NM)
                if m.has(0) and m.within(EG):
                    sp.wait_ge(e_agg, m.times(1, 1))
                    sp.dma_start(group(agg_groups, m), ys[:, m.slot(NY), :, :]).then_inc(e_stored[m.slot(NY)], 16)

            steps(sp, edges, EG, 1, NM)

            def nodes(i):
                if i.has(0) and i.within(NG):
                    n = i.slot(NX)
                    if i.has(NX):
                        sp.wait_ge(n_y, i.times(1, 1 - NX))
                    elif i.k == 0:
                        sp.wait_ge(e_turned, EG)
                    if i.last(NG):
                        sp.dma_start(xs[0:TAIL, n, :, :], x_tail).then_inc(n_x[n], 16)
                    else:
                        sp.dma_start(xs[:, n, :, :], group(x_groups, i)).then_inc(n_x[n], 16)
                m = i.plus(-NX)
                if m.has(0) and m.within(NG):
                    sp.wait_ge(n_out, m.times(1, 1))
                    if m.last(NG):
                        sp.dma_start(out_tail, ys[0:TAIL, m.slot(NY), :, :]).then_inc(n_stored[m.slot(NY)], 16)
                    else:
                        sp.dma_start(group(out_groups, m), ys[:, m.slot(NY), :, :]).then_inc(n_stored[m.slot(NY)], 16)

            steps(sp, nodes, NG, 1, NX)
            for n in range(NY):
                sp.wait_ge(n_stored[n], 16 * len(range(n, NG, NY)))

        @block.gpsimd
        def _(pool):
            pool.memset(src_q[:], N)
            pool.memset(dst_q[:], 0)
            pool.memset(prev_q[0:1, 0:1], -1.0).then_inc(s_pads, 1)
            pool.memset(onesf[:], 1.0)
            pool.memset(eps[:], EPS)
            pool.memset(onesg[:], 1.0)
            pool.memset(onese[:], 1.0)
            pool.memset(ident[:], 0.0)
            pool.memset(carry_col[:], 0.0)
            pool.memset(carry_scan[:], 0.0)
            pool.memset(b2zero[:], 0.0)
            pool.iota(iota_i[:], pattern=[[1, max(NC, HOT)]], base=0, channel_multiplier=0)
            pool.iota(edge_qi[:], pattern=[[1, QE]], base=0, channel_multiplier=QE).then_inc(s_iota, 1)
            pool.wait_ge(s_iota, 1)
            pool.memset(ones_col[:], 1.0)
            pool.memset(low_one[:, 0:1], 0.0)
            pool.memset(low_one[:, 1:2], 1.0)
            pool.tensor_copy(iota_h[:], iota_i[:, 0:HOT])
            pool.affine_select(out=ident[:], in_=ident[:], compare_op=ALU.not_equal, fill=1.0, base=0,
                               pattern=[[-1, P]], channel_multiplier=1)
            pool.affine_select(out=below[:], in_=onesf[:], compare_op=ALU.is_gt, fill=0.0, base=0,
                               pattern=[[1, P]], channel_multiplier=-1)
            pool.tensor_copy(iota_c[:], iota_i[:, 0:NC])
            pool.tensor_copy(iota_p[:], iota_i[:, 0:P])
            pool.tensor_copy(edge_q[:], edge_qi[:]).then_inc(s_iota, 1)
            pool.wait_ge(s_iota, 2)
            pool.tensor_copy(belowb[:], below[:])
            pool.tensor_copy(identb[:], ident[:]).then_inc(s_const, 1)

            pool.wait_ge(s_sorted, 1)

            def edges(i):
                if i.has(0) and i.within(EG):
                    n = i.slot(NX)
                    if i.has(NX):
                        pool.wait_ge(e_turned, i.times(1, 1 - NX))
                        pool.wait_ge(e_x[n], i.plus(-NX).visits(NX, 16 * J))
                    pool.tensor_copy(dst_now[:, n, :], columns(dst_t, i)).then_inc(e_idx, 1)
                    pool.wait_ge(e_idx, i.times(1, 1))
                    pool.sem_inc(e_issue, 1)
                    for j in range(J):
                        pool.indirect_dma_start(
                            xs[:, n, j, :], None, x,
                            bass.IndirectOffsetOnAxis(ap=dst_now[:, n, j:j + 1], axis=0)).then_inc(e_x[n], 16)

            steps(pool, edges, EG, 1, 0)
            pool.wait_ge(t_rows, 1)
            for n in range(NY):
                pool.wait_ge(e_stored[n], 16 * len(range(n, EG, NY)))

            def nodes(i):
                if i.has(0) and i.within(NG):
                    n = i.slot(NA)
                    if i.has(NA):
                        pool.wait_ge(n_xa, i.times(1, 1 - NA))
                    pool.tensor_copy(row_now[:, n, :], columns(row_idx, i))
                    pool.memset(aggs[:, n, :, :], 0.0).then_inc(n_zero, 1)
                    pool.wait_ge(n_zero, i.times(1, 1))
                    pool.sem_inc(n_issue, 1)
                    for j in range(J):
                        pool.indirect_dma_start(
                            aggs[:, n, j, :], None, agg_rows,
                            bass.IndirectOffsetOnAxis(ap=row_now[:, n, j:j + 1], axis=0),
                            bounds_check=EP - 1, oob_is_err=False).then_inc(n_agg[n], 16)

            steps(pool, nodes, NG, 1, 0)

        def transposes(source, n):
            for k in range(KD):
                for j in range(J):
                    last = nc.tensor.transpose(xt_ps[:, k, j * P:(j + 1) * P], source[:, n, j, k * P:(k + 1) * P], ident[:])
            return last

        def layer1(m, n):
            parts = [(w, v, k) for k in range(KD) for w, v in ((w1h, xth), (w1l, xth), (w1h, xtl))]
            for at, (w, v, k) in enumerate(parts):
                last = nc.tensor.matmul(hid_ps[:, m, :], w[:, k, m * P:(m + 1) * P], v[:, n, k, :],
                                        start=(at == 0), stop=(at == len(parts) - 1))
            return last

        def layer2(n, with_b2):
            parts = [(v, w, k) for k in range(KD) for v, w in ((hh, w2h), (hh, w2l), (hl, w2h))]
            for j in range(J):
                if with_b2:
                    nc.tensor.matmul(out_ps[:, j, :], ones[:], b2parts[:], start=True, stop=False)
                for at, (v, w, k) in enumerate(parts):
                    last = nc.tensor.matmul(out_ps[:, j, :], v[:, n, k, j * P:(j + 1) * P], w[:, k, :],
                                            start=(at == 0 and not with_b2), stop=(at == len(parts) - 1))
            return last

        @block.tensor
        def _(pe):
            pe.wait_ge(s_const, 1)
            pe.wait_ge(s_read, 1)
            for n, rows in enumerate((src_qf, dst_qf)):
                for h in range(QE // P):
                    last = pe.transpose(xt_ps[:, h, n * Q:(n + 1) * Q], rows[0:Q, h * P:(h + 1) * P], ident[0:Q, 0:Q])
            last.then_inc(s_turned, 1)

            for d, chunks in enumerate(CHUNKS):
                def count_digits(i):
                    if i.has(0) and i.within(EG):
                        pe.wait_ge(a_hot[d], i.times(1, 1))
                        for j in range(J):
                            for c in range(chunks):
                                last = pe.matmul(digit_count(c, i.times(J, j)), hot[:, i.slot(2), j, c * P:(c + 1) * P],
                                                 ones_col[:], start=True, stop=True, skip_group_check=True)
                        last.then_inc(a_counted[d], 1)

                steps(pe, count_digits, EG, 1, 0)
                pe.wait_ge(a_total[d], 1)
                pe.matmul(hid_ps[:, 0, 0:chunks], below[:], digit_total[:, 0:chunks], start=True, stop=True)
                pe.matmul(hid_ps[:, 1, 0:chunks], onesf[:], digit_total[:, 0:chunks], start=True, stop=True).then_inc(a_prefix[d], 1)
                pe.wait_ge(a_starts[d], 1)

                def place_edges(i):
                    m = i.plus(1)
                    if m.within(EG):
                        pe.wait_ge(b_hot[d], m.times(1, 1))
                        if m.has(1):
                            pe.wait_ge(b_copied[d], m.times(1))
                        for c in range(chunks):
                            for j in range(J):
                                last = pe.transpose(turned_ps[:, c, j * P:(j + 1) * P],
                                                    hot[:, m.slot(2), j, c * P:(c + 1) * P], identb[:])
                        last.then_inc(b_turned[d], 1)
                    if i.has(0) and i.within(EG):
                        n = i.slot(2)
                        pe.wait_ge(b_copied[d], i.times(1, 1))
                        if i.has(1):
                            pe.wait_ge(b_masked[d], i.times(1))
                        for j in range(J):
                            for c in range(chunks):
                                tile = hot_turned[:, n, c, j * P:(j + 1) * P]
                                last = pe.matmul(equal_ps[:, j, :], tile, tile, start=(c == 0), stop=(c == chunks - 1))
                        last.then_inc(b_equal[d], 1)
                    m = i.plus(-1)
                    if m.has(0) and m.within(EG):
                        n = m.slot(2)
                        pe.wait_ge(b_moves[d], m.times(1, 1))
                        for j in range(J):
                            for v in range(0, VALS, 2):
                                last = pe.matmul(moved_ps[:, v // 2, :], hot_p[:, n, j, :],
                                                 hot_t[:, n, j, v:v + 2, :].rearrange("p v t -> p (v t)"),
                                                 start=(not m.loops() and m.k == 0 and j == 0),
                                                 stop=(m.last(EG) and j == J - 1), skip_group_check=True)
                        last.then_inc(b_moved[d], 1)
                    if i.has(0) and i.within(EG):
                        n = i.slot(2)
                        pe.wait_ge(b_masked[d], i.times(1, 1))
                        if i.has(2):
                            pe.wait_ge(b_moves[d], i.times(1, -1))
                        for j in range(J):
                            for c in range(chunks):
                                pe.matmul(place_ps[:, n, j, :], hot_turned[:, n, c, j * P:(j + 1) * P],
                                          start_of(c, i.times(J, j)), start=(c == 0), stop=False)
                            last = pe.matmul(place_ps[:, n, j, :], equal[:, n, j, :], low_one[:], start=False, stop=True)
                        last.then_inc(b_place[d], 1)

                steps(pe, place_edges, EG, 1, 1)

            pe.wait_ge(s_sorted, 1)
            keys = srcf_t[:].rearrange("p (q h) -> p h q", h=QE // P)
            for h in range(QE // P):
                last = pe.transpose(xt_ps[0:Q, h, 0:P], keys[:, h, :], ident[:])
            last.then_inc(s_key_rows, 1)
            pe.wait_ge(s_row_copied, 1)
            pe.transpose(out_ps[:, 0, 0:P], carry_col[:], ident[:]).then_inc(s_row_turned, 1)
            pe.wait_ge(s_row_copied, 2)
            pe.transpose(out_ps[:, 2, 0:P], carry_scan[:], ident[:]).then_inc(s_row_turned, 1)
            pe.wait_ge(s_row_copied, 3)
            for h in range(QE // P):
                last = pe.transpose(xt_ps[:, h, 0:Q], run_q[0:Q, h * P:(h + 1) * P], ident[0:Q, 0:Q])
            last.then_inc(s_row_turned, 1)
            pe.wait_ge(s_split, 1)
            pe.wait_ge(s_cols, 1)

            def edges(i):
                j = i.plus(1)
                if j.within(EG):
                    pe.wait_ge(e_x[j.slot(NX)], j.visits(NX, 16 * J))
                    if j.has(1):
                        pe.wait_ge(e_xt, j.times(1))
                    transposes(xs, j.slot(NX)).then_inc(e_turned, 1)
                if i.has(0) and i.within(EG):
                    pe.wait_ge(e_xt, i.times(1, 1))
                    for m in range(KD):
                        if i.has(1):
                            pe.wait_ge(e_relu, i.times(KD, m + 1 - KD))
                        layer1(m, i.slot(2)).then_inc(e_layer1, 1)
                    pe.wait_ge(e_onehot, i.times(1, 1))
                    for j in range(J):
                        for h in range(2):
                            last = pe.matmul(cnt_ps[:, h, 0:HC], onep[:, i.slot(NO), j, :],
                                             onec[:, i.slot(NO), j, h * HC:(h + 1) * HC],
                                             start=(not i.loops() and i.k == 0 and j == 0),
                                             stop=(i.last(EG) and j == J - 1), skip_group_check=True)
                    last.then_inc(e_counted, 1)
                m = i.plus(-2)
                if m.has(0) and m.within(EG):
                    pe.wait_ge(e_hl, m.times(1, 1))
                    if m.has(1):
                        pe.wait_ge(e_agg, m.times(1))
                    layer2(m.slot(2), False).then_inc(e_layer2, 1)

            steps(pe, edges, EG, 1, 2)

            pe.wait_ge(t_sums, 1)
            pe.matmul(xt_ps[:, 0, 0:NG], below[:], group_sum[:], start=True, stop=True)
            pe.matmul(xt_ps[:, 1, 0:NG], onesf[:], group_sum[:], start=True, stop=True).then_inc(t_sums, 1)

            def nodes(i):
                j = i.plus(1)
                if j.within(NG):
                    pe.wait_ge(n_xa, j.times(1, 1))
                    if j.has(1):
                        pe.wait_ge(n_xt, j.times(1))
                    transposes(xa, j.slot(2)).then_inc(n_turned, 1)
                if i.has(0) and i.within(NG):
                    pe.wait_ge(n_xt, i.times(1, 1))
                    for m in range(KD):
                        if i.has(1):
                            pe.wait_ge(n_relu, i.times(KD, m + 1 - KD))
                        layer1(m, i.slot(2)).then_inc(n_layer1, 1)
                m = i.plus(-1)
                if m.has(0) and m.within(NG):
                    pe.wait_ge(n_hl, m.times(1, 1))
                    if m.has(1):
                        pe.wait_ge(n_y, m.times(1))
                    layer2(m.slot(2), True).then_inc(n_layer2, 1)

            steps(pe, nodes, NG, 1, 1)

        @block.scalar
        def _(act):
            for d, chunks in enumerate(CHUNKS):
                def copy_turned(i):
                    if i.has(0) and i.within(EG):
                        act.wait_ge(b_turned[d], i.times(1, 1))
                        if i.has(2):
                            act.wait_ge(b_place[d], i.times(1, -1))
                        nc.scalar.copy(hot_turned[:, i.slot(2), 0:chunks, :], turned_ps[:, 0:chunks, :]).then_inc(b_copied[d], 1)

                steps(act, copy_turned, EG, 1, 0)

            act.wait_ge(s_weights, 16 * (3 + KD))

            def edges(i):
                j = i.plus(1)
                if j.within(EG):
                    act.wait_ge(e_turned, j.times(1, 1))
                    if j.has(2):
                        act.wait_ge(e_layer1, j.times(KD, -KD))
                    nc.scalar.copy(xth[:, j.slot(2), :, :], xt_ps[:]).then_inc(e_high, 1)
                m = i.plus(-1)
                if m.has(0) and m.within(EG):
                    act.wait_ge(e_scan, m.times(KD, KD))
                    if m.has(2):
                        act.wait_ge(e_layer2, m.times(1, -1))
                    nc.scalar.copy(hh[:, m.slot(2), :, :], hsum[:, m.slot(2), :, :]).then_inc(e_hh, 1)
                if i.has(0) and i.within(EG):
                    for m in range(KD):
                        act.wait_ge(e_layer1, i.times(KD, m + 1))
                        if i.has(2):
                            act.wait_ge(e_scan, i.times(KD, m + 1 - 2 * KD))
                        nc.scalar.activation(hid[:, i.slot(2), m, :], hid_ps[:, m, :], ACT.Relu,
                                             bias=b1c[:, m:m + 1]).then_inc(e_relu, 1)

            steps(act, edges, EG, 1, 2)

            def nodes(i):
                j = i.plus(1)
                if j.within(NG):
                    act.wait_ge(n_turned, j.times(1, 1))
                    if j.has(2):
                        act.wait_ge(n_layer1, j.times(KD, -KD))
                    nc.scalar.copy(xth[:, j.slot(2), :, :], xt_ps[:]).then_inc(n_high, 1)
                m = i.plus(-2)
                if m.has(0) and m.within(NG):
                    n = m.slot(NY)
                    act.wait_ge(n_nmean, m.times(1, 1))
                    if m.has(1):
                        act.wait_ge(n_sq, m.times(J))
                    for j in range(J):
                        nc.scalar.activation(sq[:, j, :], ys[:, n, j, :], ACT.Square, bias=nmean[:, n, j:j + 1],
                                             accum_out=ysq[:, n, j:j + 1]).then_inc(n_sq, 1)
                    act.wait_ge(n_sq, m.times(J, J))
                    nc.scalar.activation(std[:, n, :], ysq[:, n, :], ACT.Sqrt, bias=eps[:, 0:1],
                                         scale=1.0 / D).then_inc(n_std, 1)
                if i.has(0) and i.within(NG):
                    s = i.slot(2)
                    for m in range(KD):
                        act.wait_ge(n_layer1, i.times(KD, m + 1))
                        if i.has(2):
                            act.wait_ge(n_hl, i.times(1, -1))
                        nc.scalar.activation(hid[:, s, m, :], hid_ps[:, m, :], ACT.Relu,
                                             bias=b1c[:, m:m + 1]).then_inc(n_relu, 1)
                    act.wait_ge(n_relu, i.times(KD, KD))
                    if i.has(2):
                        act.wait_ge(n_layer2, i.times(1, -1))
                    nc.scalar.copy(hh[:, s, :, :], hid[:, s, :, :]).then_inc(n_hh, 1)

            steps(act, nodes, NG, 1, 2)

        @block.vector
        def _(dve):
            chain = [0]

            def then(ins):
                chain[0] += 1
                ins.then_inc(s_sort_ops, 1)
                dve.wait_ge(s_sort_ops, chain[0])

            dve.wait_ge(s_const, 1)
            dve.wait_ge(s_lists, 64)
            dve.tensor_copy(src_qf[0:Q, :], src_q[0:Q, :])
            dve.tensor_copy(dst_qf[0:Q, :], dst_q[0:Q, :]).then_inc(s_read, 1)
            dve.wait_ge(s_weights, 16 * (3 + KD))
            dve.tensor_copy(ones[:], onesf[:])
            dve.tensor_copy(w1h[:], w1f[:])
            dve.tensor_copy(w2h[:], w2f[:])
            dve.tensor_copy(b2parts[:], b2zero[:])
            then(dve.tensor_copy(b2high[:], b2row[:]))
            dve.tensor_copy(b2parts[0:1, :], b2row[0:1, :])
            dve.tensor_tensor(b2parts[32:33, :], b2row[32:33, :], b2high[32:33, :].bitcast(F32), ALU.subtract)
            dve.tensor_tensor(w1l[:], w1f[:], w1h[:].bitcast(F32), ALU.subtract)
            dve.tensor_tensor(w2l[:], w2f[:], w2h[:].bitcast(F32), ALU.subtract).then_inc(s_split, 1)

            dve.wait_ge(s_turned, 1)
            for n, tiles in enumerate((src_t, dst_t)):
                for h in range(QE // P):
                    last = dve.tensor_copy(tiles[:].rearrange("p (q h) -> p q h", h=QE // P)[:, :, h],
                                           xt_ps[:, h, n * Q:(n + 1) * Q])
            then(last)
            dve.tensor_single_scalar(vals_i[:, 0, :], src_t[:], DIGIT, ALU.logical_shift_right)
            dve.tensor_single_scalar(vals_i[:, 1, :], src_t[:], LOW - 1, ALU.bitwise_and)
            dve.tensor_single_scalar(vals_i[:, 2, :], dst_t[:], DLOW, ALU.logical_shift_right)
            then(dve.tensor_single_scalar(vals_i[:, 3, :], dst_t[:], (1 << DLOW) - 1, ALU.bitwise_and))
            dve.tensor_copy(vals[0][:], vals_i[:]).then_inc(s_vals, 1)

            for d, chunks in enumerate(CHUNKS):
                mine, digit = vals[d], 1 - d

                def one_hot(i, n):
                    digits = columns(mine[:, digit, :], i)
                    for j in range(J):
                        last = dve.tensor_scalar(hot[:, n, j, 0:chunks * P], iota_h[:, 0:chunks * P], digits[:, j:j + 1],
                                                 None, ALU.is_equal)
                    return last

                def count_digits(i):
                    if i.has(0) and i.within(EG):
                        if i.has(2):
                            dve.wait_ge(a_counted[d], i.times(1, -1))
                        one_hot(i, i.slot(2)).then_inc(a_hot[d], 1)

                dve.wait_ge(s_vals, d + 1)
                steps(dve, count_digits, EG, 1, 0)
                dve.wait_ge(a_counted[d], EG)
                for c in range(chunks):
                    counts = cnt_ps[:, c // 2, c % 2 * ET:(c % 2 + 1) * ET]
                    last = dve.tensor_tensor_scan(digit_scan[:, c, :], onese[:], counts, 0.0, ALU.mult, ALU.add)
                then(last)
                dve.tensor_copy(digit_total[:, 0:chunks], digit_scan[:, 0:chunks, ET - 1]).then_inc(a_total[d], 1)
                for c in range(chunks):
                    counts = cnt_ps[:, c // 2, c % 2 * ET:(c % 2 + 1) * ET]
                    last = dve.tensor_tensor(digit_before[:, c, :], digit_scan[:, c, :], counts, ALU.subtract)
                then(last)
                dve.wait_ge(a_prefix[d], 1)
                then(dve.tensor_copy(digit_base[:, 0:chunks], hid_ps[:, 0, 0:chunks]))
                for c in range(1, chunks):
                    for before in range(c):
                        then(dve.tensor_tensor(digit_base[:, c:c + 1], digit_base[:, c:c + 1],
                                               hid_ps[:, 1, before:before + 1], ALU.add))
                for c in range(chunks):
                    last = dve.tensor_scalar(start_i[:, c, :], digit_before[:, c, :], digit_base[:, c:c + 1], None, ALU.add)
                then(last)
                then(dve.tensor_single_scalar(start_part[:, 0:chunks, :], start_i[:, 0:chunks, :], 8, ALU.logical_shift_right))
                then(dve.tensor_copy(starts[:, 0:chunks, :, 0], start_part[:, 0:chunks, :]))
                then(dve.tensor_single_scalar(start_part[:, 0:chunks, :], start_i[:, 0:chunks, :], 255, ALU.bitwise_and))
                dve.tensor_copy(starts[:, 0:chunks, :, 1], start_part[:, 0:chunks, :]).then_inc(a_starts[d], 1)

                def place_edges(i):
                    m = i.plus(1)
                    if m.within(EG):
                        if m.has(2):
                            dve.wait_ge(b_turned[d], m.times(1, -1))
                        one_hot(m, m.slot(2)).then_inc(b_hot[d], 1)
                    if i.has(0) and i.within(EG):
                        dve.wait_ge(b_equal[d], i.times(1, 1))
                        if i.has(2):
                            dve.wait_ge(b_place[d], i.times(1, -1))
                        dve.tensor_tensor(equal[:, i.slot(2), :, :], equal_ps, below4, ALU.mult).then_inc(b_masked[d], 1)
                    m = i.plus(-1)
                    if m.has(0) and m.within(EG):
                        n = m.slot(2)
                        dve.wait_ge(b_place[d], m.times(1, 1))
                        dve.tensor_copy(place_low[:, n, :], place_ps[:, n, :, 1]).then_inc(b_ops[d], 1)
                        dve.wait_ge(b_ops[d], m.times(4, 1))
                        dve.scalar_tensor_tensor(place[:, n, :], place_ps[:, n, :, 0], 256.0, place_low[:, n, :],
                                                 ALU.mult, ALU.add).then_inc(b_ops[d], 1)
                        dve.wait_ge(b_ops[d], m.times(4, 2))
                        dve.tensor_single_scalar(place_i[:, n, 0, :], place[:, n, :], P - 1, ALU.bitwise_and)
                        dve.tensor_single_scalar(place_i[:, n, 1, :], place[:, n, :], 7, ALU.logical_shift_right).then_inc(b_ops[d], 1)
                        dve.wait_ge(b_ops[d], m.times(4, 3))
                        dve.tensor_copy(place_f[:, n, :, :], place_i[:, n, :, :]).then_inc(b_ops[d], 1)
                        dve.wait_ge(b_ops[d], m.times(4, 4))
                        if m.has(2):
                            dve.wait_ge(b_moved[d], m.times(1, -1))
                        moving = [columns(mine[:, v, :], m) for v in range(VALS)]
                        for j in range(J):
                            dve.tensor_scalar(hot_p[:, n, j, :], iota_p[:], place_f[:, n, 0, j:j + 1], None, ALU.is_equal)
                            for v in range(VALS):
                                last = dve.tensor_scalar(hot_t[:, n, j, v, :], iota_c[:, 0:ET], place_f[:, n, 1, j:j + 1],
                                                         moving[v][:, j:j + 1], ALU.is_equal, ALU.mult)
                        last.then_inc(b_moves[d], 1)

                steps(dve, place_edges, EG, 1, 1)
                dve.wait_ge(b_moved[d], EG)
                dve.tensor_copy(vals[d + 1][:].rearrange("p (a v) t -> p a (v t)", a=2), moved_ps).then_inc(s_vals, 1)

            dve.wait_ge(s_vals, 3)
            done = vals[2]
            dve.scalar_tensor_tensor(srcf_t[:], done[:, 0, :], float(LOW), done[:, 1, :], ALU.mult, ALU.add)
            dve.scalar_tensor_tensor(src_t[:], done[:, 0, :], float(LOW), done[:, 1, :], ALU.mult, ALU.add)
            dve.scalar_tensor_tensor(dst_t[:], done[:, 2, :], float(1 << DLOW), done[:, 3, :],
                                     ALU.mult, ALU.add).then_inc(s_sorted, 1)
            dve.wait_ge(s_key_rows, 1)
            dve.tensor_copy(src_qf[0:Q, :].rearrange("q (h r) -> q h r", r=P), xt_ps[0:Q, :, 0:P]).then_inc(s_key_copied, 1)
            dve.wait_ge(s_key_copied, 1)
            chain[0] = 0

            def then(ins):
                chain[0] += 1
                ins.then_inc(s_row_ops, 1)
                dve.wait_ge(s_row_ops, chain[0])

            dve.wait_ge(s_prev, 32)
            then(dve.tensor_tensor(same_q[0:Q, :], prev_q[0:Q, :], src_qf[0:Q, :], ALU.is_equal))
            then(dve.scalar_tensor_tensor(start_q[0:Q, :], same_q[0:Q, :], 0.0, edge_q[0:Q, :], ALU.is_equal, ALU.mult))
            then(dve.tensor_tensor_scan(run_q[0:Q, :], start_q[0:Q, :], start_q[0:Q, :], 0.0, ALU.max, ALU.max))
            dve.tensor_copy(carry_col[0:Q, 0:1], run_q[0:Q, QE - 1:QE]).then_inc(s_row_copied, 1)
            dve.wait_ge(s_row_turned, 1)
            then(dve.tensor_copy(carry_row[0:1, :], out_ps[0:1, 0, 0:P]))
            dve.tensor_tensor_scan(carry_scan[0:1, 1:P], carry_row[0:1, 0:P - 1], carry_row[0:1, 0:P - 1], 0.0,
                                   ALU.max, ALU.max).then_inc(s_row_copied, 1)
            dve.wait_ge(s_row_turned, 2)
            then(dve.tensor_copy(carry_col[0:Q, 1:2], out_ps[0:Q, 2, 0:1]))
            then(dve.tensor_scalar(run_q[0:Q, :], run_q[0:Q, :], carry_col[0:Q, 1:2], -1.0, ALU.max, ALU.mult))
            dve.scalar_tensor_tensor(run_q[0:Q, :], run_q[0:Q, :], 1.0, edge_q[0:Q, :], ALU.add,
                                     ALU.add).then_inc(s_row_copied, 1)
            dve.wait_ge(s_row_turned, 3)
            for h in range(QE // P):
                last = dve.tensor_copy(cnt_t[:].rearrange("p (q h) -> p q h", h=QE // P)[:, :, h], xt_ps[:, h, 0:Q])
            last.then_inc(s_cols, 1)
            dve.tensor_scalar(part_i[:], src_t[:], SHIFT_P, P - 1, ALU.logical_shift_right, ALU.bitwise_and)
            dve.tensor_scalar(col_i[:], src_t[:], SHIFT_G, SHIFT_P, ALU.logical_shift_right, ALU.logical_shift_left)
            then(dve.tensor_scalar(col_lo[:], src_t[:], J - 1, None, ALU.bitwise_and))
            dve.tensor_copy(part_t[:], part_i[:])
            then(dve.tensor_tensor(col_t[:], col_i[:], col_lo[:], ALU.add))

            def edges(i):
                m = i.plus(-3)
                if m.has(0) and m.within(EG):
                    dve.wait_ge(e_layer2, m.times(1, 1))
                    if m.has(NY):
                        dve.wait_ge(e_stored[m.slot(NY)], m.plus(-NY).visits(NY, 16))
                    cnts = columns(cnt_t, m)
                    for j in range(J):
                        last = dve.scalar_tensor_tensor(ys[:, m.slot(NY), j, :], b2row[:], cnts[:, j:j + 1],
                                                        out_ps[:, j, :], ALU.mult, ALU.add)
                    last.then_inc(e_agg, 1)
                m = i.plus(-1)
                if m.has(0) and m.within(EG):
                    s = m.slot(2)
                    dve.wait_ge(e_same[m.slot(NM)], m.visits(NM, 16))
                    if m.has(2):
                        dve.wait_ge(e_hh, m.times(1, -1))
                    for h in range(KD):
                        dve.wait_ge(e_relu, m.times(KD, h + 1))
                        before = 0.0
                        if m.has(1):
                            dve.wait_ge(e_scan, m.times(KD, h + 1 - KD))
                            before = hsum[:, 1 - s, h, ROWS - 1:ROWS]
                        dve.tensor_tensor_scan(hsum[:, s, h, :], same[:, m.slot(NM), :], hid[:, s, h, :], before,
                                               ALU.mult, ALU.add).then_inc(e_scan, 1)
                j = i.plus(1)
                if j.within(EG):
                    if j.has(NO):
                        dve.wait_ge(e_counted, j.times(1, 1 - NO))
                    parts, cols = columns(part_t, j), columns(col_t, j)
                    for t in range(J):
                        dve.tensor_scalar(onep[:, j.slot(NO), t, :], iota_p[:], parts[:, t:t + 1], None, ALU.is_equal)
                        last = dve.tensor_scalar(onec[:, j.slot(NO), t, :], iota_c[:], cols[:, t:t + 1], None, ALU.is_equal)
                    last.then_inc(e_onehot, 1)
                    dve.wait_ge(e_high, j.times(1, 1))
                    dve.tensor_tensor(xtl[:, j.slot(2), :, :], xt_ps[:], xth[:, j.slot(2), :, :].bitcast(F32),
                                      ALU.subtract).then_inc(e_xt, 1)
                if m.has(0) and m.within(EG):
                    dve.wait_ge(e_hh, m.times(1, 1))
                    dve.tensor_tensor(hl[:, s, :, :], hsum[:, s, :, :], hh[:, s, :, :].bitcast(F32),
                                      ALU.subtract).then_inc(e_hl, 1)

            steps(dve, edges, EG, 1, 3)

            chain[0] = 0

            def then(ins):
                chain[0] += 1
                ins.then_inc(t_ops, 1)
                dve.wait_ge(t_ops, chain[0])

            dve.wait_ge(e_counted, EG)
            flat = count[:].rearrange("p g j -> p (g j)")
            dve.tensor_copy(flat[:, 0:HC], cnt_ps[:, 0, 0:HC])
            then(dve.tensor_copy(flat[:, HC:NC], cnt_ps[:, 1, 0:HC]))
            then(dve.tensor_copy(upto[:, :, 0], count[:, :, 0]))
            for j in range(1, J):
                then(dve.tensor_tensor(upto[:, :, j], upto[:, :, j - 1], count[:, :, j], ALU.add))
            dve.tensor_copy(group_sum[:], upto[:, :, J - 1]).then_inc(t_sums, 1)
            then(dve.tensor_scalar(count[:], count[:], 0.0, float(1 << 20), ALU.is_equal, ALU.mult))
            then(dve.scalar_tensor_tensor(rowf[:], upto[:], -1.0, count[:], ALU.add, ALU.add))
            dve.wait_ge(t_sums, 2)
            then(dve.tensor_tensor_scan(group_scan[:], onesg[:], xt_ps[:, 1, 0:NG], 0.0, ALU.mult, ALU.add))
            then(dve.tensor_tensor(base[:], group_scan[:], xt_ps[:, 1, 0:NG], ALU.subtract))
            then(dve.tensor_tensor(base[:], base[:], xt_ps[:, 0, 0:NG], ALU.add))
            for j in range(J):
                last = dve.tensor_tensor(rowf[:, :, j], rowf[:, :, j], base[:], ALU.add)
            then(last)
            dve.tensor_copy(row_idx[:].rearrange("p (g j) -> p g j", j=J), rowf[:]).then_inc(t_rows, 1)

            def nodes(i):
                m = i.plus(-2)
                if m.has(0) and m.within(NG):
                    n = m.slot(NY)
                    dve.wait_ge(n_layer2, m.times(1, 1))
                    if m.has(NY):
                        dve.wait_ge(n_stored[n], m.plus(-NY).visits(NY, 16))
                    for j in range(J):
                        last = dve.scalar_tensor_tensor(ys[:, n, j, :], out_ps[:, j, :], 1.0, xs[:, m.slot(NX), j, :], ALU.mult,
                                                        ALU.add, accum_out=ysum[:, n, j:j + 1])
                    last.then_inc(n_y, 1)
                    dve.wait_ge(n_y, m.times(1, 1))
                    dve.tensor_scalar(nmean[:, n, :], ysum[:, n, :], -1.0 / D, None, ALU.mult).then_inc(n_nmean, 1)
                m = i.plus(-1)
                if m.has(0) and m.within(NG):
                    s = m.slot(2)
                    dve.wait_ge(n_hh, m.times(1, 1))
                    dve.tensor_tensor(hl[:, s, :, :], hid[:, s, :, :], hh[:, s, :, :].bitcast(F32),
                                      ALU.subtract).then_inc(n_hl, 1)
                j = i.plus(1)
                if j.has(0) and j.within(NG):
                    dve.wait_ge(n_high, j.times(1, 1))
                    dve.tensor_tensor(xtl[:, j.slot(2), :, :], xt_ps[:], xth[:, j.slot(2), :, :].bitcast(F32),
                                      ALU.subtract).then_inc(n_xt, 1)
                m = i.plus(-2)
                if m.has(0) and m.within(NG):
                    n = m.slot(NY)
                    dve.wait_ge(n_std, m.times(1, 1))
                    dve.reciprocal(rstd[:, n, :], std[:, n, :]).then_inc(n_rstd, 1)
                    dve.wait_ge(n_rstd, m.times(1, 1))
                    for j in range(J):
                        last = dve.tensor_scalar(ys[:, n, j, :], ys[:, n, j, :], nmean[:, n, j:j + 1], rstd[:, n, j:j + 1],
                                                 ALU.add, ALU.mult)
                    last.then_inc(n_out, 1)
                j = i.plus(2)
                if j.within(NG):
                    dve.wait_ge(n_x[j.slot(NX)], j.visits(NX, 16))
                    dve.wait_ge(n_agg[j.slot(NA)], j.visits(NA, 16 * J))
                    if j.has(2):
                        dve.wait_ge(n_turned, j.times(1, -1))
                    dve.tensor_tensor(xa[:, j.slot(2), :, :], xs[:, j.slot(NX), :, :], aggs[:, j.slot(NA), :, :],
                                      ALU.add).then_inc(n_xa, 1)

            steps(dve, nodes, NG, 2, 2)


_INS = ["x", "src", "dst", "L0_gnn_w1", "L0_gnn_b1", "L0_gnn_w2", "L0_gnn_b2"]


def kernel(**inputs):
    import numpy as _np
    import concourse.bacc as _bacc
    from concourse import mybir as _mybir
    from concourse.bass_utils import run_bass_kernel_spmd as _run

    nc = _bacc.Bacc("TRN2", target_bir_lowering=False, num_devices=1)
    arrays, args = {}, []
    for name in _INS:
        a = _np.ascontiguousarray(inputs[name])
        arrays[f"in_{name}_dram"] = a
        args.append(nc.dram_tensor(f"in_{name}_dram", a.shape, _mybir.dt.from_np(a.dtype), kind="ExternalInput").ap())
    shape = inputs["x"].shape
    args.append(nc.dram_tensor("out_0_dram", shape, F32, kind="ExternalOutput").ap())
    gnn_kernel(nc, *args)
    r = _run(nc, [arrays], core_ids=[0])
    return r.results[0]["out_0_dram"]
```

```python
from contextlib import ExitStack

import concourse.bass as bass
from concourse import mybir

P = 128
ALU = mybir.AluOpType
ACT = mybir.ActivationFunctionType
F32 = mybir.dt.float32
F32R = mybir.dt.float32r
BF16 = mybir.dt.bfloat16
F16 = mybir.dt.float16
I32 = mybir.dt.int32

U = 6


class Step:

    def __init__(self, turn, k):
        self.turn, self.k = turn, k

    def plus(self, n):
        return Step(self.turn, self.k + n)

    def slot(self, slots):
        return self.k % slots

    def within(self, groups):
        return not isinstance(self.turn, int) or 0 <= self.k < groups

    def has(self, n):
        if isinstance(self.turn, int):
            return self.k >= n
        assert U + self.k >= n, "not so in the loop's first turn"
        return True

    def loops(self):
        return not isinstance(self.turn, int)

    def last(self, groups):
        return isinstance(self.turn, int) and self.k == groups - 1

    def times(self, per, more=0):
        return self.turn * (U * per) + (self.k * per + more)

    def visits(self, slots, per):
        return self.turn * (U // slots * per) + (self.k // slots + 1) * per


def steps(engine, body, groups, ahead, behind):
    turns = (groups - ahead) // U
    for n in range(-ahead, U):
        body(Step(0, n))
    with engine.Fori(1, turns) as turn:
        for k in range(U):
            body(Step(turn, k))
    for n in range(turns * U, groups + behind):
        body(Step(0, n))


def gnn_kernel(nc, x, src, dst, w1, b1, w2, b2, out):
    N, D = x.shape
    E, = src.shape
    KD = D // P
    J = 4
    ROWS = J * P
    EG = -(-E // ROWS)
    EP = EG * ROWS
    ET = EG * J
    NG = -(-N // ROWS)
    TAIL = (N - (NG - 1) * ROWS) // J
    NC = NG * J
    QE = 2 * P
    Q = EP // QE
    SHIFT_P, SHIFT_G = 2, 9
    DIGIT = 8
    LOW = 1 << DIGIT
    CHUNKS = (LOW // P, -(-(N // LOW + 1) // P))
    HOT = max(CHUNKS) * P
    ROW0 = 2 * EG - 1
    EPS = 1e-5
    assert D == KD * P and J == 1 << SHIFT_P and ROWS == 1 << SHIFT_G and TAIL * J == N - (NG - 1) * ROWS
    assert Q <= P and ROW0 < P and ET < 256 and HOT <= 512 and ET * 2 <= 512 and EP < 1 << 16 and N < 1 << 24 and NG * ROWS > N

    with ExitStack() as ctx:
        def sb(name, shape, dt=F32):
            return ctx.enter_context(nc.sbuf_tensor(name, shape, dt))

        def sem(name):
            return ctx.enter_context(nc.semaphore(name))

        def ps(name, shape, dt=F32):
            return ctx.enter_context(nc.psum_tensor(name, shape, dt))

        moved = [nc.dram_tensor(f"moved{d}", (EP, 2), I32, kind="Internal").ap() for d in range(2)]
        same_row = nc.dram_tensor("same_row", (EP,), F32, kind="Internal").ap()
        agg_rows = nc.dram_tensor("agg_rows", (EP, D), F32, kind="Internal").ap()

        JA = 1
        NX, NA, NY, NM, NO, NP = U, 3, 3, 3, 2, 3

        w1f, w2f = sb("w1f", [P, KD, D]), sb("w2f", [P, KD, D])
        w1h, w1l = sb("w1h", [P, KD, D], F32R), sb("w1l", [P, KD, D], F32R)
        w2h, w2l = sb("w2h", [P, KD, D], F32R), sb("w2l", [P, KD, D], F32R)
        b1c = sb("b1c", [P, KD])
        b2row = sb("b2row", [P, D])
        b2parts = sb("b2parts", [P, D], F32R)
        ones = sb("ones", [P, P], F32R)
        onesf = sb("onesf", [P, P])
        below = sb("below", [P, P])
        ident = sb("ident", [P, P])
        b2zero = sb("b2zero", [P, D])
        b2high = sb("b2high", [P, D], F32R)
        onesc = onesf[:, 0:1]
        eps = sb("eps", [P, 1])
        WIDE = max(NC, HOT, ET + 1)
        iota_i, iota = sb("iota_i", [P, WIDE], I32), sb("iota", [P, WIDE], F16)

        src_t, dst_t = sb("src_t", [P, ET], I32), sb("dst_t", [P, ET], I32)
        pair = sb("pair", [P, ET, 2], I32)
        pair_q, prev_q = sb("pair_q", [P, QE, 2], I32), sb("prev_q", [P, QE, 2], I32)
        src_qf, dst_qf, same_q = sb("src_qf", [P, QE]), sb("dst_qf", [P, QE]), sb("same_q", [P, QE])
        run_q = sb("run_q", [P, QE])
        edge_q, edge_qi = sb("edge_q", [P, QE]), sb("edge_qi", [P, QE], I32)
        start_q = sb("start_q", [P, QE])
        carry_col, carry_row, carry_scan = sb("carry_col", [P, P]), sb("carry_row", [P, P]), sb("carry_scan", [P, P])
        cnt_t = sb("cnt_t", [P, ET])
        part_i, col_i, col_lo = (sb(n, [P, ET], I32) for n in ("part_i", "col_i", "col_lo"))
        part_t, col_t = sb("part_t", [P, ET]), sb("col_t", [P, ET])

        digit_i, digit = sb("digit_i", [P, ET], I32), sb("digit", [P, ET])
        equal = sb("equal", [P, 2, J, P], BF16)
        place_now, pair_now = sb("place_now", [P, NP, J], I32), sb("pair_now", [P, NP, J, 2], I32)
        place_sum = sb("place_sum", [P, 2, J])
        digit_total = sb("digit_total", [P, HOT // P])
        digit_base = sb("digit_base", [P, HOT // P])
        starts = sb("starts", [P, HOT // P, ET, 2], BF16)
        belowb, identb = sb("belowb", [P, P], BF16), sb("identb", [P, P], BF16)
        low_one = sb("low_one", [P, 2], BF16)
        band = sb("band", [P, ROW0 + P], BF16)
        turn_i, odd_i, row_tile = sb("turn_i", [P, 1], I32), sb("odd_i", [P, 1], I32), sb("row_tile", [P, 2])
        tile_counts = sb("tile_counts", [P, 2, HOT], BF16)
        ahead = sb("ahead", [P, 2, ET + 1], BF16)

        count = sb("count", [P, NG, J])
        upto = sb("upto", [P, NG, J])
        group_sum = sb("group_sum", [P, NG])
        dst_now = sb("dst_now", [P, NX, J], I32)
        row_now = sb("row_now", [P, 3, J], I32)
        onesg = sb("onesg", [P, NG])
        group_scan = sb("group_scan", [P, NG])
        base = sb("base", [P, NG])
        rowf = sb("rowf", [P, NG, J])
        row_idx = sb("row_idx", [P, NC], I32)

        xs = sb("xs", [P, NX, J, D])
        aggs = sb("aggs", [P, NA, J, D])
        xa = sb("xa", [P, 2, J, D])
        xth, xtl = sb("xth", [P, 2, KD, ROWS], F32R), sb("xtl", [P, 2, KD, ROWS], F32R)
        hid = sb("hid", [P, 2, KD, ROWS])
        hsum = sb("hsum", [P, 2, KD, ROWS])
        hh, hl = sb("hh", [P, 2, KD, ROWS], F32R), sb("hl", [P, 2, KD, ROWS], F32R)
        same = sb("same", [P, NM, ROWS])
        onep, onec = sb("onep", [P, NO, J, P], BF16), sb("onec", [P, NO, J, NC], BF16)
        ys = sb("ys", [P, NY, J, D])
        sq = sb("sq", [P, J, D])
        ysum, nmean, ysq = sb("ysum", [P, NY, J]), sb("nmean", [P, NY, J]), sb("ysq", [P, NY, J])
        shift = sb("shift", [P, NY, J])
        std, rstd = sb("std", [P, NY, J]), sb("rstd", [P, NY, J])

        def over(ring, shape, dt, at=0):
            size = 1
            for n in shape:
                size *= n
            dims = " ".join("abc"[:len(ring.shape) - 1])
            flat = ring[:].rearrange(f"p {dims} -> p ({dims})").bitcast(dt)
            dims = " ".join("abcd"[:len(shape)])
            return flat[:, at:at + size].rearrange(f"p ({dims}) -> p {dims}", **dict(zip("abcd", shape)))

        hot = over(aggs, [3, J, HOT], BF16)
        hot_turned = over(xs, [3, HOT // P, J * P], BF16)
        start_i, start_part = (over(xa, [HOT // P, ET], I32, n * HOT // P * ET) for n in range(2))

        xt_ps = ps("xt_ps", [P, KD, ROWS])
        hid_ps = ps("hid_ps", [P, KD, ROWS])
        out_ps = ps("out_ps", [P, J, D])
        cnt_ps = ps("cnt_ps", [P, 2, ROWS])
        turned_ps = xt_ps[:].rearrange("p k r -> p (k r)").bitcast(BF16).rearrange("p (c r) -> p c r", r=J * P)
        equal_ps = hid_ps[:, 0, :].rearrange("p (j e) -> p j e", j=J)
        place_ps = cnt_ps[:, :, 0:2 * J].rearrange("p n (j v) -> p n j v", j=J)
        node_ps = out_ps[:].rearrange("p (a b) d -> p a (b d)", a=2)
        before_ps = out_ps[:]
        base_ps = cnt_ps[:, 0, 0:HOT // P]

        below4 = belowb[:, None, :].broadcast_to([P, J, P])

        def to_row(i, r):
            at = i.times(2, r)
            return band[:, at:at + P] if isinstance(at, int) else band[:, bass.ds(at, P)]

        def start_of(c, t):
            return starts[:, c, t, :] if isinstance(t, int) else starts[:, c, bass.ds(t, 1), :].rearrange("p a v -> p (a v)")

        HC = NC // 2

        s_pads = sem("s_pads")
        s_weights, s_lists = sem("s_weights"), sem("s_lists")
        s_const, s_iota, s_split = sem("s_const"), sem("s_iota"), sem("s_split")
        s_band, s_fill = sem("s_band"), sem("s_fill")
        a_hot, a_counted, a_counts, a_before, a_total, a_base, a_starts = (
            [sem(f"{n}{d}") for d in range(2)]
            for n in ("a_hot", "a_counted", "a_counts", "a_before", "a_total", "a_base", "a_starts"))
        b_hot, b_turned, b_copied, b_equal, b_masked, b_place, b_sum, b_now = (
            [sem(f"{n}{d}") for d in range(2)]
            for n in ("b_hot", "b_turned", "b_copied", "b_equal", "b_masked", "b_place", "b_sum", "b_now"))
        b_moved = [[sem(f"b_moved{d}_{n}") for n in range(NP)] for d in range(2)]
        s_rows, s_read, s_turned = ([sem(f"{n}{d}") for d in range(2)] for n in ("s_rows", "s_read", "s_turned"))
        s_sorted = sem("s_sorted")
        s_sort_ops = sem("s_sort_ops")
        s_row_ops, s_row_turned, s_row_copied = sem("s_row_ops"), sem("s_row_turned"), sem("s_row_copied")
        s_same_out = sem("s_same_out")
        e_idx = sem("e_idx")
        b_issue, e_issue, n_issue = sem("b_issue"), sem("e_issue"), sem("n_issue")
        e_x = [sem(f"e_x{n}") for n in range(NX)]
        e_same = [sem(f"e_same{n}") for n in range(NM)]
        e_turned, e_high, e_xt = sem("e_turned"), sem("e_high"), sem("e_xt")
        e_layer1, e_relu, e_scan, e_hh, e_hl = sem("e_layer1"), sem("e_relu"), sem("e_scan"), sem("e_hh"), sem("e_hl")
        e_layer2, e_agg = sem("e_layer2"), sem("e_agg")
        e_stored = [sem(f"e_stored{n}") for n in range(NY)]
        c_onehot, c_counted = sem("c_onehot"), sem("c_counted")
        t_sums, t_rows = sem("t_sums"), sem("t_rows")
        n_x = [sem(f"n_x{n}") for n in range(NX)]
        n_zero = sem("n_zero")
        n_agg = [sem(f"n_agg{n}") for n in range(NA)]
        n_xa, n_turned, n_high, n_xt = sem("n_xa"), sem("n_turned"), sem("n_high"), sem("n_xt")
        n_layer1, n_relu, n_hh, n_hl, n_layer2 = (
            sem("n_layer1"), sem("n_relu"), sem("n_hh"), sem("n_hl"), sem("n_layer2"))
        n_y, n_nmean, n_sq, n_std, n_rstd, n_shift, n_out, n_out_act = (
            sem("n_y"), sem("n_nmean"), sem("n_sq"), sem("n_std"), sem("n_rstd"), sem("n_shift"), sem("n_out"),
            sem("n_out_act"))
        n_stored = [sem(f"n_stored{n}") for n in range(NY)]

        block = ctx.enter_context(nc.Block())

        full = N - (NG - 1) * ROWS
        x_groups = x[0:(NG - 1) * ROWS, :].rearrange("(g p j) d -> g p j d", p=P, j=J)
        out_groups = out[0:(NG - 1) * ROWS, :].rearrange("(g p j) d -> g p j d", p=P, j=J)
        x_tail = x[N - full:N, :].rearrange("(p j) d -> p j d", j=J)
        out_tail = out[N - full:N, :].rearrange("(p j) d -> p j d", j=J)
        agg_groups = agg_rows.rearrange("(g j p) d -> g p j d", p=P, j=J)
        same_groups = same_row.rearrange("(g r) -> g r", r=ROWS)

        def pairs(step):
            i = step.times(J)
            return pair[:, i:i + J, :] if isinstance(i, int) else pair[:, bass.ds(i, J), :]

        def columns(table, step):
            i = step.times(J)
            return table[:, i:i + J] if isinstance(i, int) else table[:, bass.ds(i, J)]

        def group(view, step):
            i = step.times(1)
            return view[i] if isinstance(i, int) else view[bass.ds(i, 1)].rearrange("a p j d -> p (a j) d")

        @block.sync
        def _(sp):
            sp.wait_ge(s_pads, 1)
            whole = E // ET
            rest = E - whole * ET
            for tile, lst in ((src_t, src), (dst_t, dst)):
                sp.dma_start(tile[0:whole, :], lst[0:whole * ET].rearrange("(p t) -> p t", t=ET)).then_inc(s_lists, 16)
                sp.dma_start(tile[whole:whole + 1, 0:rest], lst[whole * ET:E].rearrange("(p t) -> p t", p=1)).then_inc(s_lists, 16)
            for tile, w in ((w1f, w1), (w2f, w2)):
                sp.dma_start(tile[:], w.rearrange("(k p) n -> p k n", p=P)).then_inc(s_weights, 16)
            for k in range(KD):
                sp.dma_start(b1c[:, k:k + 1], b1[k * P:(k + 1) * P].rearrange("(p a) -> p a", a=1)).then_inc(s_weights, 16)
            sp.dma_start(b2row[:], b2.rearrange("(a n) -> a n", a=1).broadcast_to([P, D])).then_inc(s_weights, 16)
            for d in range(2):
                for n in range(NP):
                    sp.wait_ge(b_moved[d][n], 16 * J * len(range(n, EG, NP)))
                sp.dma_start(pair_q[0:Q, :, :], moved[d].rearrange("(q r) v -> q r v", r=QE)).then_inc(s_rows[d], 16)
            sp.dma_start(prev_q[0:1, 1:QE, :], moved[1][0:QE - 1, :].rearrange("(q r) v -> q r v", q=1)).then_inc(s_rows[1], 16)
            sp.dma_start(prev_q[1:Q, :, :], moved[1][QE - 1:EP - 1, :].rearrange("(q r) v -> q r v", r=QE)).then_inc(s_rows[1], 16)
            sp.wait_ge(s_row_ops, 1)
            sp.dma_start(same_row.rearrange("(q r) -> q r", r=QE), same_q[0:Q, :]).then_inc(s_same_out, 16)
            sp.wait_ge(s_same_out, 16)

            def edges(i):
                if i.has(0) and i.within(EG):
                    if i.has(NM):
                        sp.wait_ge(e_scan, i.times(KD, KD * (1 - NM)))
                    n = i.slot(NM)
                    g = i.times(1)
                    row = same_groups[g:g + 1, :] if isinstance(g, int) else same_groups[bass.ds(g, 1), :]
                    sp.dma_start(same[:, n, :], row.broadcast_to([P, ROWS])).then_inc(e_same[n], 16)
                if not i.loops() and i.k == EG:
                    sp.wait_ge(e_turned, EG)
                    for n in range(NX):
                        sp.dma_start(xs[:, n, :, :], x_groups[n]).then_inc(n_x[n], 16)
                m = i.plus(-NM)
                if m.has(0) and m.within(EG):
                    sp.wait_ge(e_agg, m.times(1, 1))
                    sp.dma_start(group(agg_groups, m), ys[:, m.slot(NY), :, :]).then_inc(e_stored[m.slot(NY)], 16)

            steps(sp, edges, EG, 1, NM)

            def nodes(i):
                if i.has(NX) and i.within(NG):
                    n = i.slot(NX)
                    sp.wait_ge(n_y, i.times(1, 1 - NX))
                    if i.last(NG):
                        sp.dma_start(xs[0:TAIL, n, :, :], x_tail).then_inc(n_x[n], 16)
                    else:
                        sp.dma_start(xs[:, n, :, :], group(x_groups, i)).then_inc(n_x[n], 16)
                m = i.plus(-NX)
                if m.has(0) and m.within(NG):
                    sp.wait_ge(n_out, m.times(1, 1))
                    sp.wait_ge(n_out_act, m.times(1, 1))
                    if m.last(NG):
                        sp.dma_start(out_tail, ys[0:TAIL, m.slot(NY), :, :]).then_inc(n_stored[m.slot(NY)], 16)
                    else:
                        sp.dma_start(group(out_groups, m), ys[:, m.slot(NY), :, :]).then_inc(n_stored[m.slot(NY)], 16)

            steps(sp, nodes, NG, 1, NX)
            for n in range(NY):
                sp.wait_ge(n_stored[n], 16 * len(range(n, NG, NY)))

        @block.gpsimd
        def _(pool):
            pool.memset(src_t[:], N)
            pool.memset(dst_t[:], 0)
            pool.memset(prev_q[0:1, 0:1, :], -1).then_inc(s_pads, 1)
            pool.iota(iota_i[:], pattern=[[1, WIDE]], base=0, channel_multiplier=0)
            pool.iota(turn_i[:], pattern=[[0, 1]], base=ROW0, channel_multiplier=-1)
            pool.memset(band[:], 0.0).then_inc(s_iota, 1)
            pool.wait_ge(s_iota, 1)
            pool.memset(band[:, ROW0:ROW0 + 1], 1.0).then_inc(s_band, 1)
            pool.memset(onesf[:], 1.0)
            pool.memset(eps[:], EPS)
            pool.memset(onesg[:], 1.0)
            pool.memset(ident[:], 0.0)
            pool.memset(carry_col[:], 0.0)
            pool.memset(carry_scan[:], 0.0)
            pool.memset(b2zero[:], 0.0)
            pool.memset(low_one[:, 0:1], 0.0)
            pool.memset(low_one[:, 1:2], 1.0)
            pool.iota(edge_qi[:], pattern=[[1, QE]], base=0, channel_multiplier=QE).then_inc(s_fill, 1)
            pool.wait_ge(s_fill, 1)
            pool.affine_select(out=ident[:], in_=ident[:], compare_op=ALU.not_equal, fill=1.0, base=0,
                               pattern=[[-1, P]], channel_multiplier=1)
            pool.affine_select(out=below[:], in_=onesf[:], compare_op=ALU.is_gt, fill=0.0, base=0,
                               pattern=[[1, P]], channel_multiplier=-1)
            pool.tensor_copy(edge_q[:], edge_qi[:]).then_inc(s_fill, 1)
            pool.wait_ge(s_fill, 2)
            pool.tensor_copy(belowb[:], below[:])
            pool.tensor_copy(identb[:], ident[:]).then_inc(s_const, 1)

            for d in range(2):
                def move(i):
                    if i.has(0) and i.within(EG):
                        n = i.slot(NP)
                        pool.wait_ge(b_now[d], i.times(1, 1))
                        pool.sem_inc(b_issue, 1)
                        for j in range(J):
                            pool.indirect_dma_start(
                                moved[d], bass.IndirectOffsetOnAxis(ap=place_now[:, n, j:j + 1], axis=0),
                                pair_now[:, n, j, :], None).then_inc(b_moved[d][n], 16)

                steps(pool, move, EG, 1, 0)

            pool.wait_ge(s_sorted, 1)

            def edges(i):
                if i.has(0) and i.within(EG):
                    n = i.slot(NX)
                    if i.has(NX):
                        pool.wait_ge(e_turned, i.times(1, 1 - NX))
                        pool.wait_ge(e_x[n], i.plus(-NX).visits(NX, 16 * J))
                    pool.tensor_copy(dst_now[:, n, :], pairs(i)[:, :, 1]).then_inc(e_idx, 1)
                    pool.wait_ge(e_idx, i.times(1, 1))
                    pool.sem_inc(e_issue, 1)
                    for j in range(J):
                        pool.indirect_dma_start(
                            xs[:, n, j, :], None, x,
                            bass.IndirectOffsetOnAxis(ap=dst_now[:, n, j:j + 1], axis=0)).then_inc(e_x[n], 16)

            steps(pool, edges, EG, 1, 0)
            pool.wait_ge(t_rows, 1)

            def nodes(i):
                m = i.plus(1)
                if m.within(NG):
                    n = m.slot(NA)
                    if m.has(NA):
                        pool.wait_ge(n_xa, m.times(1, 1 - NA))
                    pool.tensor_copy(row_now[:, n, :], columns(row_idx, m))
                    pool.memset(aggs[:, n, :, :], 0.0).then_inc(n_zero, 1)
                if i.has(0) and i.within(NG):
                    n = i.slot(NA)
                    if not i.loops() and i.k == 0:
                        for s in range(NY):
                            pool.wait_ge(e_stored[s], 16 * len(range(s, EG, NY)))
                    pool.wait_ge(n_zero, i.times(1, 1))
                    pool.sem_inc(n_issue, 1)
                    for j in range(J):
                        pool.indirect_dma_start(
                            aggs[:, n, j, :], None, agg_rows,
                            bass.IndirectOffsetOnAxis(ap=row_now[:, n, j:j + 1], axis=0),
                            bounds_check=EP - 1, oob_is_err=False).then_inc(n_agg[n], 16)

            steps(pool, nodes, NG, 1, 0)

        def transposes(source, n):
            for k in range(KD):
                for j in range(J):
                    last = nc.tensor.transpose(xt_ps[:, k, j * P:(j + 1) * P], source[:, n, j, k * P:(k + 1) * P], ident[:])
            return last

        def layer1(m, n):
            parts = [(w, v, k) for k in range(KD) for w, v in ((w1h, xth), (w1l, xth), (w1h, xtl))]
            for at, (w, v, k) in enumerate(parts):
                last = nc.tensor.matmul(hid_ps[:, m, :], w[:, k, m * P:(m + 1) * P], v[:, n, k, :],
                                        start=(at == 0), stop=(at == len(parts) - 1))
            return last

        def layer2(n, with_b2):
            parts = [(v, w, k) for k in range(KD) for v, w in ((hh, w2h), (hh, w2l), (hl, w2h))]
            for j in range(J):
                if with_b2:
                    nc.tensor.matmul(out_ps[:, j, :], ones[:], b2parts[:], start=True, stop=False)
                for at, (v, w, k) in enumerate(parts):
                    last = nc.tensor.matmul(out_ps[:, j, :], v[:, n, k, j * P:(j + 1) * P], w[:, k, :],
                                            start=(at == 0 and not with_b2), stop=(at == len(parts) - 1))
            return last

        @block.tensor
        def _(pe):
            pe.wait_ge(s_band, 1)
            for d, chunks in enumerate(CHUNKS):
                def count_digits(i):
                    if i.has(0) and i.within(EG):
                        pe.wait_ge(a_hot[d], i.times(1, 1))
                        for j in range(J):
                            last = pe.matmul(cnt_ps[:, j // 2, 0:chunks * P], to_row(i, j % 2), hot[:, i.slot(3), j, 0:chunks * P],
                                             start=(not i.loops() and i.k == 0 and j % 2 == 0),
                                             stop=(i.last(EG) and j % 2 == 1), skip_group_check=True)
                        last.then_inc(a_counted[d], 1)

                steps(pe, count_digits, EG, 1, 0)
                pe.wait_ge(a_counts[d], 1)
                for c in range(chunks):
                    for h in range(2):
                        last = pe.matmul(before_ps[:, c, 0:ET + 1], tile_counts[:, h, c * P:(c + 1) * P], ahead[:, h, :],
                                         start=(h == 0), stop=(h == 1))
                last.then_inc(a_before[d], 1)
                pe.wait_ge(s_const, 1)
                pe.wait_ge(a_total[d], 1)
                for c in range(chunks):
                    for low in range(c):
                        pe.matmul(base_ps[:, c:c + 1], onesf[:], digit_total[:, low:low + 1], start=(low == 0), stop=False)
                    last = pe.matmul(base_ps[:, c:c + 1], below[:], digit_total[:, c:c + 1], start=(c == 0), stop=True)
                last.then_inc(a_base[d], 1)

                def place_edges(i):
                    m = i.plus(1)
                    if m.has(0) and m.within(EG):
                        pe.wait_ge(b_hot[d], m.times(1, 1))
                        if m.has(1):
                            pe.wait_ge(b_copied[d], m.times(1))
                        for c in range(chunks):
                            for j in range(J):
                                last = pe.transpose(turned_ps[:, c, j * P:(j + 1) * P],
                                                    hot[:, m.slot(3), j, c * P:(c + 1) * P], identb[:])
                        last.then_inc(b_turned[d], 1)
                    if i.has(0) and i.within(EG):
                        pe.wait_ge(b_copied[d], i.times(1, 1))
                        if i.has(1):
                            pe.wait_ge(b_masked[d], i.times(1))
                        for j in range(J):
                            for c in range(chunks):
                                tile = hot_turned[:, i.slot(3), c, j * P:(j + 1) * P]
                                last = pe.matmul(equal_ps[:, j, :], tile, tile, start=(c == 0), stop=(c == chunks - 1))
                        last.then_inc(b_equal[d], 1)
                    m = i.plus(-1)
                    if m.has(0) and m.within(EG):
                        n = m.slot(2)
                        if not m.loops() and m.k == 0:
                            pe.wait_ge(a_starts[d], 1)
                        pe.wait_ge(b_masked[d], m.times(1, 1))
                        if m.has(2):
                            pe.wait_ge(b_now[d], m.times(1, -1))
                        for j in range(J):
                            for c in range(chunks):
                                pe.matmul(place_ps[:, n, j, :], hot_turned[:, m.slot(3), c, j * P:(j + 1) * P],
                                          start_of(c, m.times(J, j)), start=(c == 0), stop=False)
                            last = pe.matmul(place_ps[:, n, j, :], equal[:, n, j, :], low_one[:], start=False, stop=True)
                        last.then_inc(b_place[d], 1)
                        if d == 0:
                            pe.wait_ge(c_onehot, m.times(1, 1))
                            for j in range(J):
                                for h in range(2):
                                    last = pe.matmul(node_ps[:, h, 0:HC], onep[:, m.slot(NO), j, :],
                                                     onec[:, m.slot(NO), j, h * HC:(h + 1) * HC],
                                                     start=(not m.loops() and m.k == 0 and j == 0),
                                                     stop=(m.last(EG) and j == J - 1), skip_group_check=True)
                            last.then_inc(c_counted, 1)

                steps(pe, place_edges, EG, 2, 1)
                if d == 1:
                    pe.wait_ge(t_sums, 1)
                    pe.matmul(cnt_ps[:, 0, 0:NG], below[:], group_sum[:], start=True, stop=True)
                    pe.matmul(cnt_ps[:, 1, 0:NG], onesf[:], group_sum[:], start=True, stop=True).then_inc(t_sums, 1)
                pe.wait_ge(s_read[d], 1)
                for n, rows in enumerate((src_qf, dst_qf)):
                    for h in range(QE // P):
                        last = pe.transpose(xt_ps[:, h, n * Q:(n + 1) * Q], rows[0:Q, h * P:(h + 1) * P], ident[0:Q, 0:Q])
                last.then_inc(s_turned[d], 1)

            pe.wait_ge(s_row_copied, 1)
            pe.transpose(out_ps[:, 0, 0:P], carry_col[:], ident[:]).then_inc(s_row_turned, 1)
            pe.wait_ge(s_row_copied, 2)
            pe.transpose(out_ps[:, 2, 0:P], carry_scan[:], ident[:]).then_inc(s_row_turned, 1)
            pe.wait_ge(s_row_copied, 3)
            for h in range(QE // P):
                last = pe.transpose(cnt_ps[:, h, 0:Q], run_q[0:Q, h * P:(h + 1) * P], ident[0:Q, 0:Q])
            last.then_inc(s_row_turned, 1)
            pe.wait_ge(s_split, 1)
            pe.wait_ge(s_sorted, 1)

            def edges(i):
                j = i.plus(1)
                if j.within(EG):
                    pe.wait_ge(e_x[j.slot(NX)], j.visits(NX, 16 * J))
                    if j.has(1):
                        pe.wait_ge(e_xt, j.times(1))
                    transposes(xs, j.slot(NX)).then_inc(e_turned, 1)
                if i.has(0) and i.within(EG):
                    pe.wait_ge(e_xt, i.times(1, 1))
                    for m in range(KD):
                        if i.has(1):
                            pe.wait_ge(e_relu, i.times(KD, m + 1 - KD))
                        layer1(m, i.slot(2)).then_inc(e_layer1, 1)
                m = i.plus(-2)
                if m.has(0) and m.within(EG):
                    pe.wait_ge(e_hl, m.times(1, 1))
                    if m.has(1):
                        pe.wait_ge(e_agg, m.times(1))
                    layer2(m.slot(2), False).then_inc(e_layer2, 1)

            steps(pe, edges, EG, 1, 2)

            def nodes(i):
                j = i.plus(1)
                if j.within(NG):
                    pe.wait_ge(n_xa, j.times(1, 1))
                    if j.has(1):
                        pe.wait_ge(n_xt, j.times(1))
                    transposes(xa, j.slot(2)).then_inc(n_turned, 1)
                if i.has(0) and i.within(NG):
                    pe.wait_ge(n_xt, i.times(1, 1))
                    for m in range(KD):
                        if i.has(1):
                            pe.wait_ge(n_relu, i.times(KD, m + 1 - KD))
                        layer1(m, i.slot(2)).then_inc(n_layer1, 1)
                m = i.plus(-1)
                if m.has(0) and m.within(NG):
                    pe.wait_ge(n_hl, m.times(1, 1))
                    if m.has(1):
                        pe.wait_ge(n_y, m.times(1))
                    layer2(m.slot(2), True).then_inc(n_layer2, 1)

            steps(pe, nodes, NG, 1, 1)

        @block.scalar
        def _(act):
            for d, chunks in enumerate(CHUNKS):
                def copy_turned(i):
                    if i.has(0) and i.within(EG):
                        act.wait_ge(b_turned[d], i.times(1, 1))
                        if i.has(3):
                            act.wait_ge(b_place[d], i.times(1, -2))
                        nc.scalar.copy(hot_turned[:, i.slot(3), 0:chunks, :], turned_ps[:, 0:chunks, :]).then_inc(b_copied[d], 1)

                steps(act, copy_turned, EG, 1, 0)

            act.wait_ge(s_weights, 16 * (3 + KD))

            def edges(i):
                j = i.plus(1)
                if j.within(EG):
                    act.wait_ge(e_turned, j.times(1, 1))
                    if j.has(2):
                        act.wait_ge(e_layer1, j.times(KD, -KD))
                    nc.scalar.copy(xth[:, j.slot(2), :, :], xt_ps[:]).then_inc(e_high, 1)
                m = i.plus(-1)
                if m.has(0) and m.within(EG):
                    act.wait_ge(e_scan, m.times(KD, KD))
                    if m.has(2):
                        act.wait_ge(e_layer2, m.times(1, -1))
                    nc.scalar.copy(hh[:, m.slot(2), :, :], hsum[:, m.slot(2), :, :]).then_inc(e_hh, 1)
                if i.has(0) and i.within(EG):
                    for m in range(KD):
                        act.wait_ge(e_layer1, i.times(KD, m + 1))
                        if i.has(2):
                            act.wait_ge(e_scan, i.times(KD, m + 1 - 2 * KD))
                        nc.scalar.activation(hid[:, i.slot(2), m, :], hid_ps[:, m, :], ACT.Relu,
                                             bias=b1c[:, m:m + 1]).then_inc(e_relu, 1)

            steps(act, edges, EG, 1, 2)

            def nodes(i):
                j = i.plus(1)
                if j.within(NG):
                    act.wait_ge(n_turned, j.times(1, 1))
                    if j.has(2):
                        act.wait_ge(n_layer1, j.times(KD, -KD))
                    nc.scalar.copy(xth[:, j.slot(2), :, :], xt_ps[:]).then_inc(n_high, 1)
                m = i.plus(-2)
                if m.has(0) and m.within(NG):
                    n = m.slot(NY)
                    act.wait_ge(n_nmean, m.times(1, 1))
                    if m.has(1):
                        act.wait_ge(n_sq, m.times(J))
                    for j in range(J):
                        nc.scalar.activation(sq[:, j, :], ys[:, n, j, :], ACT.Square, bias=nmean[:, n, j:j + 1],
                                             accum_out=ysq[:, n, j:j + 1]).then_inc(n_sq, 1)
                    act.wait_ge(n_sq, m.times(J, J))
                    nc.scalar.activation(std[:, n, :], ysq[:, n, :], ACT.Sqrt, bias=eps[:, 0:1],
                                         scale=1.0 / D).then_inc(n_std, 1)
                if i.has(0) and i.within(NG):
                    s = i.slot(2)
                    for m in range(KD):
                        act.wait_ge(n_layer1, i.times(KD, m + 1))
                        if i.has(2):
                            act.wait_ge(n_hl, i.times(1, -1))
                        nc.scalar.activation(hid[:, s, m, :], hid_ps[:, m, :], ACT.Relu,
                                             bias=b1c[:, m:m + 1]).then_inc(n_relu, 1)
                    act.wait_ge(n_relu, i.times(KD, KD))
                    if i.has(2):
                        act.wait_ge(n_layer2, i.times(1, -1))
                    nc.scalar.copy(hh[:, s, :, :], hid[:, s, :, :]).then_inc(n_hh, 1)
                m = i.plus(-2)
                if m.has(0) and m.within(NG):
                    n = m.slot(NY)
                    act.wait_ge(n_shift, m.times(1, 1))
                    for j in range(JA):
                        last = nc.scalar.activation(ys[:, n, j, :], ys[:, n, j, :], ACT.Identity, bias=shift[:, n, j:j + 1],
                                                    scale=rstd[:, n, j:j + 1])
                    last.then_inc(n_out_act, 1)

            steps(act, nodes, NG, 1, 2)

        @block.vector
        def _(dve):
            chain = [0]

            def then(ins):
                chain[0] += 1
                ins.then_inc(s_sort_ops, 1)
                dve.wait_ge(s_sort_ops, chain[0])

            dve.wait_ge(s_iota, 1)
            dve.tensor_copy(iota[:], iota_i[:])
            then(dve.tensor_single_scalar(odd_i[:], turn_i[:], 1, ALU.bitwise_and))
            then(dve.scalar_tensor_tensor(row_tile[:, 0:1], turn_i[:], 2.0, odd_i[:], ALU.mult, ALU.subtract))
            then(dve.tensor_scalar(row_tile[:, 1:2], row_tile[:, 0:1], 2.0, None, ALU.add))
            for h in range(2):
                dve.tensor_scalar(ahead[:, h, :], iota[:, 0:ET + 1], row_tile[:, h:h + 1], None, ALU.is_gt)

            def prepare_moves():
                dve.tensor_scalar(part_i[:], src_t[:], SHIFT_P, P - 1, ALU.logical_shift_right, ALU.bitwise_and)
                dve.tensor_scalar(col_i[:], src_t[:], SHIFT_G, SHIFT_P, ALU.logical_shift_right, ALU.logical_shift_left)
                dve.tensor_scalar(col_lo[:], src_t[:], J - 1, None, ALU.bitwise_and)
                dve.tensor_copy(pair[:, :, 0], src_t[:])
                then(dve.tensor_copy(pair[:, :, 1], dst_t[:]))
                dve.tensor_copy(part_t[:], part_i[:])
                then(dve.tensor_tensor(col_t[:], col_i[:], col_lo[:], ALU.add))

            def split_weights():
                dve.wait_ge(s_weights, 16 * (3 + KD))
                dve.tensor_copy(ones[:], onesf[:])
                dve.tensor_copy(w1h[:], w1f[:])
                dve.tensor_copy(w2h[:], w2f[:])
                dve.tensor_copy(b2parts[:], b2zero[:])
                then(dve.tensor_copy(b2high[:], b2row[:]))
                dve.tensor_copy(b2parts[0:1, :], b2row[0:1, :])
                dve.tensor_tensor(b2parts[32:33, :], b2row[32:33, :], b2high[32:33, :].bitcast(F32), ALU.subtract)
                dve.tensor_tensor(w1l[:], w1f[:], w1h[:].bitcast(F32), ALU.subtract)
                dve.tensor_tensor(w2l[:], w2f[:], w2h[:].bitcast(F32), ALU.subtract).then_inc(s_split, 1)

            def node_table():
                then(dve.tensor_copy(upto[:, :, 0], count[:, :, 0]))
                for j in range(1, J):
                    then(dve.tensor_tensor(upto[:, :, j], upto[:, :, j - 1], count[:, :, j], ALU.add))
                dve.tensor_copy(group_sum[:], upto[:, :, J - 1]).then_inc(t_sums, 1)
                then(dve.tensor_scalar(count[:], count[:], 0.0, float(1 << 20), ALU.is_equal, ALU.mult))
                then(dve.scalar_tensor_tensor(rowf[:], upto[:], -1.0, count[:], ALU.add, ALU.add))
                dve.wait_ge(t_sums, 2)
                then(dve.tensor_tensor_scan(group_scan[:], onesg[:], cnt_ps[:, 1, 0:NG], 0.0, ALU.mult, ALU.add))
                then(dve.tensor_tensor(base[:], group_scan[:], cnt_ps[:, 1, 0:NG], ALU.subtract))
                then(dve.tensor_tensor(base[:], base[:], cnt_ps[:, 0, 0:NG], ALU.add))
                for j in range(J):
                    last = dve.tensor_tensor(rowf[:, :, j], rowf[:, :, j], base[:], ALU.add)
                then(last)
                dve.tensor_copy(row_idx[:].rearrange("p (g j) -> p g j", j=J), rowf[:]).then_inc(t_rows, 1)

            for d, chunks in enumerate(CHUNKS):
                if d == 0:
                    dve.wait_ge(s_lists, 64)
                    then(dve.tensor_single_scalar(digit_i[:], src_t[:], LOW - 1, ALU.bitwise_and))
                else:
                    then(dve.tensor_single_scalar(digit_i[:], pair[:, :, 0], DIGIT, ALU.logical_shift_right))
                then(dve.tensor_copy(digit[:], digit_i[:]))

                def one_hot(i, n):
                    digits = columns(digit, i)
                    for j in range(J):
                        last = dve.tensor_scalar(hot[:, n, j, 0:chunks * P], iota[:, 0:chunks * P], digits[:, j:j + 1],
                                                 None, ALU.is_equal)
                    return last

                def count_digits(i):
                    if i.has(0) and i.within(EG):
                        if i.has(3):
                            dve.wait_ge(a_counted[d], i.times(1, -2))
                        one_hot(i, i.slot(3)).then_inc(a_hot[d], 1)

                steps(dve, count_digits, EG, 1, 0)
                dve.wait_ge(a_counted[d], EG)
                dve.tensor_copy(tile_counts[:, :, 0:chunks * P], cnt_ps[:, :, 0:chunks * P]).then_inc(a_counts[d], 1)
                dve.wait_ge(a_before[d], 1)
                dve.tensor_copy(digit_total[:, 0:chunks], before_ps[:, 0:chunks, ET]).then_inc(a_total[d], 1)
                for n in range(2):
                    one_hot(Step(0, n), n).then_inc(b_hot[d], 1)
                dve.wait_ge(a_base[d], 1)
                then(dve.tensor_copy(digit_base[:, 0:chunks], base_ps[:, 0:chunks]))
                for c in range(chunks):
                    last = dve.tensor_scalar(start_i[:, c, :], before_ps[:, c, 0:ET], digit_base[:, c:c + 1], None, ALU.add)
                then(last)
                then(dve.tensor_single_scalar(start_part[:, 0:chunks, :], start_i[:, 0:chunks, :], 0xFF00, ALU.bitwise_and))
                then(dve.tensor_copy(starts[:, 0:chunks, :, 0], start_part[:, 0:chunks, :]))
                then(dve.tensor_single_scalar(start_part[:, 0:chunks, :], start_i[:, 0:chunks, :], 255, ALU.bitwise_and))
                dve.tensor_copy(starts[:, 0:chunks, :, 1], start_part[:, 0:chunks, :]).then_inc(a_starts[d], 1)
                if d == 0:
                    prepare_moves()
                    dve.wait_ge(s_const, 1)

                def place_edges(i):
                    m = i.plus(2)
                    if m.has(2) and m.within(EG):
                        if m.has(3):
                            dve.wait_ge(b_turned[d], m.times(1, -2))
                        one_hot(m, m.slot(3)).then_inc(b_hot[d], 1)
                    if i.has(0) and i.within(EG):
                        dve.wait_ge(b_equal[d], i.times(1, 1))
                        if i.has(2):
                            dve.wait_ge(b_place[d], i.times(1, -1))
                        dve.tensor_tensor(equal[:, i.slot(2), :, :], equal_ps, below4, ALU.mult).then_inc(b_masked[d], 1)
                    m = i.plus(-2)
                    if m.has(0) and m.within(EG):
                        n = m.slot(NP)
                        dve.wait_ge(b_place[d], m.times(1, 1))
                        if m.has(NP):
                            dve.wait_ge(b_moved[d][n], m.plus(-NP).visits(NP, 16 * J))
                        dve.tensor_reduce(place_sum[:, m.slot(2), :], place_ps[:, m.slot(2), :, :], mybir.AxisListType.X,
                                          ALU.add).then_inc(b_sum[d], 1)
                        dve.tensor_copy(pair_now[:, n, :, :], pairs(m))
                        dve.wait_ge(b_sum[d], m.times(1, 1))
                        dve.tensor_copy(place_now[:, n, :], place_sum[:, m.slot(2), :]).then_inc(b_now[d], 1)
                    if d == 0 and i.has(0) and i.within(EG):
                        n = i.slot(NO)
                        if i.has(NO):
                            dve.wait_ge(c_counted, i.times(1, 1 - NO))
                        parts, cols = columns(part_t, i), columns(col_t, i)
                        for j in range(J):
                            dve.tensor_scalar(onep[:, n, j, :], iota[:, 0:P], parts[:, j:j + 1], None, ALU.is_equal)
                            last = dve.tensor_scalar(onec[:, n, j, :], iota[:, 0:NC], cols[:, j:j + 1], None, ALU.is_equal)
                        last.then_inc(c_onehot, 1)

                steps(dve, place_edges, EG, 2, 2)
                if d == 0:
                    dve.wait_ge(c_counted, EG)
                    flat = count[:].rearrange("p g j -> p (g j)")
                    for h in range(2):
                        last = dve.tensor_copy(flat[:, h * HC:(h + 1) * HC], node_ps[:, h, 0:HC])
                    then(last)
                else:
                    node_table()
                    split_weights()
                dve.wait_ge(s_rows[d], 16 if d == 0 else 48)
                dve.tensor_copy(src_qf[0:Q, :], pair_q[0:Q, :, 0])
                dve.tensor_copy(dst_qf[0:Q, :], pair_q[0:Q, :, 1]).then_inc(s_read[d], 1)
                dve.wait_ge(s_turned[d], 1)
                tiles = pair[:].rearrange("p (q h) v -> p q h v", h=QE // P)
                for n in range(2):
                    for h in range(QE // P):
                        last = dve.tensor_copy(tiles[:, :, h, n], xt_ps[:, h, n * Q:(n + 1) * Q])
                if d == 0:
                    then(last)
                else:
                    last.then_inc(s_sorted, 1)
            chain[0] = 0

            def then(ins):
                chain[0] += 1
                ins.then_inc(s_row_ops, 1)
                dve.wait_ge(s_row_ops, chain[0])

            then(dve.tensor_tensor(same_q[0:Q, :], prev_q[0:Q, :, 0], pair_q[0:Q, :, 0], ALU.is_equal))
            then(dve.scalar_tensor_tensor(start_q[0:Q, :], same_q[0:Q, :], 0.0, edge_q[0:Q, :], ALU.is_equal, ALU.mult))
            then(dve.tensor_tensor_scan(run_q[0:Q, :], start_q[0:Q, :], start_q[0:Q, :], 0.0, ALU.max, ALU.max))
            dve.tensor_copy(carry_col[0:Q, 0:1], run_q[0:Q, QE - 1:QE]).then_inc(s_row_copied, 1)
            dve.wait_ge(s_row_turned, 1)
            then(dve.tensor_copy(carry_row[0:1, :], out_ps[0:1, 0, 0:P]))
            dve.tensor_tensor_scan(carry_scan[0:1, 1:P], carry_row[0:1, 0:P - 1], carry_row[0:1, 0:P - 1], 0.0,
                                   ALU.max, ALU.max).then_inc(s_row_copied, 1)
            dve.wait_ge(s_row_turned, 2)
            then(dve.tensor_copy(carry_col[0:Q, 1:2], out_ps[0:Q, 2, 0:1]))
            then(dve.tensor_scalar(run_q[0:Q, :], run_q[0:Q, :], carry_col[0:Q, 1:2], -1.0, ALU.max, ALU.mult))
            dve.scalar_tensor_tensor(run_q[0:Q, :], run_q[0:Q, :], 1.0, edge_q[0:Q, :], ALU.add,
                                     ALU.add).then_inc(s_row_copied, 1)
            dve.wait_ge(s_row_turned, 3)
            for h in range(QE // P):
                last = dve.tensor_copy(cnt_t[:].rearrange("p (q h) -> p q h", h=QE // P)[:, :, h], cnt_ps[:, h, 0:Q])
            then(last)

            def edges(i):
                m = i.plus(-3)
                if m.has(0) and m.within(EG):
                    dve.wait_ge(e_layer2, m.times(1, 1))
                    if m.has(NY):
                        dve.wait_ge(e_stored[m.slot(NY)], m.plus(-NY).visits(NY, 16))
                    cnts = columns(cnt_t, m)
                    for j in range(J):
                        last = dve.scalar_tensor_tensor(ys[:, m.slot(NY), j, :], b2row[:], cnts[:, j:j + 1],
                                                        out_ps[:, j, :], ALU.mult, ALU.add)
                    last.then_inc(e_agg, 1)
                m = i.plus(-1)
                if m.has(0) and m.within(EG):
                    s = m.slot(2)
                    dve.wait_ge(e_same[m.slot(NM)], m.visits(NM, 16))
                    if m.has(2):
                        dve.wait_ge(e_hh, m.times(1, -1))
                    for h in range(KD):
                        dve.wait_ge(e_relu, m.times(KD, h + 1))
                        before = 0.0
                        if m.has(1):
                            dve.wait_ge(e_scan, m.times(KD, h + 1 - KD))
                            before = hsum[:, 1 - s, h, ROWS - 1:ROWS]
                        dve.tensor_tensor_scan(hsum[:, s, h, :], same[:, m.slot(NM), :], hid[:, s, h, :], before,
                                               ALU.mult, ALU.add).then_inc(e_scan, 1)
                j = i.plus(1)
                if j.within(EG):
                    dve.wait_ge(e_high, j.times(1, 1))
                    dve.tensor_tensor(xtl[:, j.slot(2), :, :], xt_ps[:], xth[:, j.slot(2), :, :].bitcast(F32),
                                      ALU.subtract).then_inc(e_xt, 1)
                if m.has(0) and m.within(EG):
                    dve.wait_ge(e_hh, m.times(1, 1))
                    dve.tensor_tensor(hl[:, s, :, :], hsum[:, s, :, :], hh[:, s, :, :].bitcast(F32),
                                      ALU.subtract).then_inc(e_hl, 1)

            steps(dve, edges, EG, 1, 3)

            def nodes(i):
                m = i.plus(-2)
                if m.has(0) and m.within(NG):
                    n = m.slot(NY)
                    dve.wait_ge(n_layer2, m.times(1, 1))
                    if m.has(NY):
                        dve.wait_ge(n_stored[n], m.plus(-NY).visits(NY, 16))
                    for j in range(J):
                        last = dve.scalar_tensor_tensor(ys[:, n, j, :], out_ps[:, j, :], 1.0, xs[:, m.slot(NX), j, :], ALU.mult,
                                                        ALU.add, accum_out=ysum[:, n, j:j + 1])
                    last.then_inc(n_y, 1)
                    dve.wait_ge(n_y, m.times(1, 1))
                    dve.tensor_scalar(nmean[:, n, :], ysum[:, n, :], -1.0 / D, None, ALU.mult).then_inc(n_nmean, 1)
                m = i.plus(-1)
                if m.has(0) and m.within(NG):
                    s = m.slot(2)
                    dve.wait_ge(n_hh, m.times(1, 1))
                    dve.tensor_tensor(hl[:, s, :, :], hid[:, s, :, :], hh[:, s, :, :].bitcast(F32),
                                      ALU.subtract).then_inc(n_hl, 1)
                j = i.plus(1)
                if j.has(0) and j.within(NG):
                    dve.wait_ge(n_high, j.times(1, 1))
                    dve.tensor_tensor(xtl[:, j.slot(2), :, :], xt_ps[:], xth[:, j.slot(2), :, :].bitcast(F32),
                                      ALU.subtract).then_inc(n_xt, 1)
                j = i.plus(2)
                if j.within(NG):
                    dve.wait_ge(n_x[j.slot(NX)], j.visits(NX, 16))
                    dve.wait_ge(n_agg[j.slot(NA)], j.visits(NA, 16 * J))
                    if j.has(2):
                        dve.wait_ge(n_turned, j.times(1, -1))
                    dve.tensor_tensor(xa[:, j.slot(2), :, :], xs[:, j.slot(NX), :, :], aggs[:, j.slot(NA), :, :],
                                      ALU.add).then_inc(n_xa, 1)
                m = i.plus(-2)
                if m.has(0) and m.within(NG):
                    n = m.slot(NY)
                    dve.wait_ge(n_std, m.times(1, 1))
                    dve.reciprocal(rstd[:, n, :], std[:, n, :]).then_inc(n_rstd, 1)
                    dve.wait_ge(n_rstd, m.times(1, 1))
                    dve.tensor_tensor(shift[:, n, :], nmean[:, n, :], rstd[:, n, :], ALU.mult).then_inc(n_shift, 1)
                    for j in range(JA, J):
                        last = dve.tensor_scalar(ys[:, n, j, :], ys[:, n, j, :], nmean[:, n, j:j + 1], rstd[:, n, j:j + 1],
                                                 ALU.add, ALU.mult)
                    last.then_inc(n_out, 1)

            steps(dve, nodes, NG, 2, 2)


_INS = ["x", "src", "dst", "L0_gnn_w1", "L0_gnn_b1", "L0_gnn_w2", "L0_gnn_b2"]


def kernel(**inputs):
    import numpy as _np
    import concourse.bacc as _bacc
    from concourse import mybir as _mybir
    from concourse.bass_utils import run_bass_kernel_spmd as _run

    nc = _bacc.Bacc("TRN2", target_bir_lowering=False, num_devices=1)
    arrays, args = {}, []
    for name in _INS:
        a = _np.ascontiguousarray(inputs[name])
        arrays[f"in_{name}_dram"] = a
        args.append(nc.dram_tensor(f"in_{name}_dram", a.shape, _mybir.dt.from_np(a.dtype), kind="ExternalInput").ap())
    shape = inputs["x"].shape
    args.append(nc.dram_tensor("out_0_dram", shape, F32, kind="ExternalOutput").ap())
    gnn_kernel(nc, *args)
    r = _run(nc, [arrays], core_ids=[0])
    return r.results[0]["out_0_dram"]
```
